# Optimizing a Trainium2 kernel written in Bass

```python
import numpy as np
import jax
import jax.numpy as jnp

def _softmax(x, axis=-1):
    return jax.nn.softmax(x, axis=axis)

def _gelu(x):
    return jax.nn.gelu(x, approximate=True)

def _silu(x):
    return jax.nn.silu(x)

def _sigmoid(x):
    return jax.nn.sigmoid(x)

def _layernorm(x, axis=-1, eps=1e-05):
    m = jnp.mean(x, axis=axis, keepdims=True)
    v = jnp.var(x, axis=axis, keepdims=True)
    return (x - m) / jnp.sqrt(v + eps)

def _scatter_add(tgt, idx, src, axis=0):
    return tgt.at[idx].add(src)

def _segment_sum(src, seg, n):
    return jax.ops.segment_sum(src, seg, n)
kernel_name = 'mk_hybrid_d1_jaxref_r4_3130ac'

def setup_inputs(seed: int=0):
    np.random.seed(seed)
    _w = jnp.asarray

    def _L0_attn_a_setup():
        import jax, jax.numpy as jnp
        import numpy as np
        H = 16
        EPS = 1e-06
        key = jax.random.key(seed)
        ks = jax.random.split(key, 5)
        B, N, D = (4, 1024, 256)
        x = jax.random.normal(ks[0], (B, N, D), dtype=jnp.float32)
        q = jax.random.normal(ks[1], (D,), dtype=jnp.float32)
        k = jax.random.normal(ks[2], (D,), dtype=jnp.float32)
        log_decay = jax.random.normal(ks[3], (H,), dtype=jnp.float32)
        norm_weight = jnp.ones((D,), dtype=jnp.float32)
        o_w = jax.random.normal(ks[4], (D, D), dtype=jnp.float32) * 0.02
        return {'x': x, 'q': q, 'k': k, 'log_decay': log_decay, 'norm_weight': norm_weight, 'o_w': o_w}
    _L0_attn_a_in = _L0_attn_a_setup()

    def _L0_attn_b_setup():
        import jax, jax.numpy as jnp
        import numpy as np
        NUM_HEAD = 16
        HEAD_DIM = 64
        RES_DIM = 256
        LN_EPS = 1e-05

        def _layer_norm(x, w, b):
            mu = jnp.mean(x, axis=-1, keepdims=True)
            var = jnp.var(x, axis=-1, keepdims=True)
            return (x - mu) * jax.lax.rsqrt(var + LN_EPS) * w + b
        key = jax.random.key(seed)
        k1, k2, k3 = jax.random.split(key, 3)
        slen, bsz = (512, 4)
        x = jax.random.normal(k1, (slen, bsz, RES_DIM), dtype=jnp.float32)
        w_qkv = jax.random.normal(k2, (NUM_HEAD * 3 * HEAD_DIM, RES_DIM), dtype=jnp.float32) * (1.0 / np.sqrt(RES_DIM))
        w_out = jax.random.normal(k3, (RES_DIM, NUM_HEAD * HEAD_DIM), dtype=jnp.float32) * (1.0 / np.sqrt(NUM_HEAD * HEAD_DIM))
        ln_w = jnp.ones((RES_DIM,), dtype=jnp.float32)
        ln_b = jnp.zeros((RES_DIM,), dtype=jnp.float32)
        return {'x': x, 'w_qkv': w_qkv, 'w_out': w_out, 'ln_w': ln_w, 'ln_b': ln_b}
    _L0_attn_b_in = _L0_attn_b_setup()

    def _L0_ffn_setup():
        import jax, jax.numpy as jnp
        import numpy as np
        B, C, D, O = (4, 1024, 256, 256)
        PROJ = 64
        RANKS = [1, 2, 4, 8]
        E = len(RANKS)
        CLAMP_MAX = float(np.log(1.0 / 0.01))

        def _l2norm(v, axis):
            return v / jnp.maximum(jnp.linalg.norm(v, axis=axis, keepdims=True), 1e-12)
        key = jax.random.key(seed)
        ks = jax.random.split(key, 16)
        inp = {'x': jax.random.normal(ks[0], (B, C, D), dtype=jnp.float32), 'W': jax.random.normal(ks[1], (O, D), dtype=jnp.float32) / np.sqrt(D), 'Wp': jax.random.normal(ks[2], (PROJ, D), dtype=jnp.float32) / np.sqrt(D), 'bp': jnp.zeros((PROJ,), dtype=jnp.float32), 'sim': jax.random.normal(ks[3], (PROJ, E), dtype=jnp.float32) * 0.01, 'temp': jnp.full((1,), np.log(1.0 / 0.5), dtype=jnp.float32)}
        for i, r in enumerate(RANKS):
            inp[f'Wd{i}'] = jax.random.normal(ks[4 + 2 * i], (r, D), dtype=jnp.float32) / r
            inp[f'Wu{i}'] = jax.random.normal(ks[5 + 2 * i], (O, r), dtype=jnp.float32) * 0.01
        return inp
    _L0_ffn_in = _L0_ffn_setup()
    _d = {'L0_attn_a_x': _L0_attn_a_in['x'], 'L0_attn_a_q': _L0_attn_a_in['q'], 'L0_attn_a_k': _L0_attn_a_in['k'], 'L0_attn_a_log_decay': _L0_attn_a_in['log_decay'], 'L0_attn_a_norm_weight': _L0_attn_a_in['norm_weight'], 'L0_attn_a_o_w': _L0_attn_a_in['o_w'], 'L0_attn_b_w_qkv': _L0_attn_b_in['w_qkv'], 'L0_attn_b_w_out': _L0_attn_b_in['w_out'], 'L0_attn_b_ln_w': _L0_attn_b_in['ln_w'], 'L0_attn_b_ln_b': _L0_attn_b_in['ln_b'], 'L0_ffn_W': _L0_ffn_in['W'], 'L0_ffn_Wp': _L0_ffn_in['Wp'], 'L0_ffn_bp': _L0_ffn_in['bp'], 'L0_ffn_sim': _L0_ffn_in['sim'], 'L0_ffn_temp': _L0_ffn_in['temp'], 'L0_ffn_Wd0': _L0_ffn_in['Wd0'], 'L0_ffn_Wu0': _L0_ffn_in['Wu0'], 'L0_ffn_Wd1': _L0_ffn_in['Wd1'], 'L0_ffn_Wu1': _L0_ffn_in['Wu1'], 'L0_ffn_Wd2': _L0_ffn_in['Wd2'], 'L0_ffn_Wu2': _L0_ffn_in['Wu2'], 'L0_ffn_Wd3': _L0_ffn_in['Wd3'], 'L0_ffn_Wu3': _L0_ffn_in['Wu3']}
    _x0 = _d['L0_attn_a_x']
    _d['L0_attn_a_x'] = jax.random.normal(jax.random.fold_in(jax.random.key(seed), 1), (4, 2048, 256), dtype=_x0.dtype)
    del _x0
    return _d

def reference(L0_attn_a_x, L0_attn_a_q, L0_attn_a_k, L0_attn_a_log_decay, L0_attn_a_norm_weight, L0_attn_a_o_w, L0_attn_b_w_qkv, L0_attn_b_w_out, L0_attn_b_ln_w, L0_attn_b_ln_b, L0_ffn_W, L0_ffn_Wp, L0_ffn_bp, L0_ffn_sim, L0_ffn_temp, L0_ffn_Wd0, L0_ffn_Wu0, L0_ffn_Wd1, L0_ffn_Wu1, L0_ffn_Wd2, L0_ffn_Wu2, L0_ffn_Wd3, L0_ffn_Wu3):

    def _L0_attn_a_ref(x, q, k, log_decay, norm_weight, o_w):
        import jax, jax.numpy as jnp
        import numpy as np
        H = 16
        EPS = 1e-06
        b, n, dm = x.shape
        dh = dm // H
        qh = q.reshape(H, dh)
        kh = k.reshape(H, dh)
        v = x.reshape(b, n, H, dh)
        lam = jax.nn.sigmoid(log_decay)

        def step(S, v_t):
            S = lam[None, :, None, None] * S + kh[None, :, :, None] * v_t[:, :, None, :]
            o_t = jnp.einsum('hd,bhdv->bhv', qh, S)
            return (S, o_t)
        S0 = jnp.zeros((b, H, dh, dh), dtype=x.dtype)
        _, o = jax.lax.scan(step, S0, jnp.moveaxis(v, 1, 0))
        o = jnp.moveaxis(o, 0, 1).reshape(b, n, dm)
        o = o * jax.lax.rsqrt(jnp.mean(o * o, axis=-1, keepdims=True) + EPS) * norm_weight
        return o @ o_w.T

    def _L0_attn_b_ref(x, w_qkv, w_out, ln_w, ln_b):
        import jax, jax.numpy as jnp
        import numpy as np
        NUM_HEAD = 16
        HEAD_DIM = 64
        RES_DIM = 256
        LN_EPS = 1e-05

        def _layer_norm(x, w, b):
            mu = jnp.mean(x, axis=-1, keepdims=True)
            var = jnp.var(x, axis=-1, keepdims=True)
            return (x - mu) * jax.lax.rsqrt(var + LN_EPS) * w + b
        slen, bsz, _ = x.shape
        scale = 1.0 / np.sqrt(RES_DIM).astype(np.float32)
        x_in = _layer_norm(x, ln_w, ln_b)
        qkv = x_in @ w_qkv.T
        qkv = qkv.reshape(slen, bsz, NUM_HEAD, 3 * HEAD_DIM)
        q, k, v = jnp.split(qkv, 3, axis=-1)
        scores = jnp.einsum('ibnd,jbnd->ijbn', q, k) * scale
        attn = jax.nn.softmax(scores, axis=1)
        attn_out = jnp.einsum('ijbn,jbnd->ibnd', attn, v)
        attn_out = attn_out.reshape(slen, bsz, NUM_HEAD * HEAD_DIM)
        attn_out = attn_out @ w_out.T
        return x + attn_out

    def _L0_ffn_ref(x, W, Wp, bp, sim, temp, Wd0, Wu0, Wd1, Wu1, Wd2, Wu2, Wd3, Wu3):
        import jax, jax.numpy as jnp
        import numpy as np
        B, C, D, O = (4, 1024, 256, 256)
        PROJ = 64
        RANKS = [1, 2, 4, 8]
        E = len(RANKS)
        CLAMP_MAX = float(np.log(1.0 / 0.01))

        def _l2norm(v, axis):
            return v / jnp.maximum(jnp.linalg.norm(v, axis=axis, keepdims=True), 1e-12)
        base = jnp.einsum('bcd,od->bco', x, W)
        xf = x.reshape(-1, x.shape[-1])
        proj = _l2norm(xf @ Wp.T + bp, axis=1)
        simn = _l2norm(sim, axis=0)
        scale = jnp.exp(jnp.minimum(temp, CLAMP_MAX))
        logits = proj @ simn * scale
        lw = jax.nn.softmax(logits, axis=1)
        top1 = jnp.argmax(lw, axis=1)
        ret = jnp.where(jnp.arange(E)[None, :] == top1[:, None], lw, 0.0)
        ret = ret.reshape(x.shape[0], x.shape[1], E)
        downs = (Wd0, Wd1, Wd2, Wd3)
        ups = (Wu0, Wu1, Wu2, Wu3)
        l = jnp.stack([jnp.einsum('bcr,or->bco', jnp.einsum('bcd,rd->bcr', x, d), u) for d, u in zip(downs, ups)], axis=2)
        res = jnp.sum(ret[..., None] * l, axis=2)
        return base + res
    x = L0_attn_a_x
    x = x + _L0_attn_a_ref(_layernorm(x, axis=-1), L0_attn_a_q, L0_attn_a_k, L0_attn_a_log_decay, L0_attn_a_norm_weight, L0_attn_a_o_w)
    x = x + _L0_ffn_ref(_layernorm(x, axis=-1), L0_ffn_W, L0_ffn_Wp, L0_ffn_bp, L0_ffn_sim, L0_ffn_temp, L0_ffn_Wd0, L0_ffn_Wu0, L0_ffn_Wd1, L0_ffn_Wu1, L0_ffn_Wd2, L0_ffn_Wu2, L0_ffn_Wd3, L0_ffn_Wu3)
    x = x + _L0_attn_b_ref(_layernorm(x, axis=-1), L0_attn_b_w_qkv, L0_attn_b_w_out, L0_attn_b_ln_w, L0_attn_b_ln_b)
    x = x + _L0_ffn_ref(_layernorm(x, axis=-1), L0_ffn_W, L0_ffn_Wp, L0_ffn_bp, L0_ffn_sim, L0_ffn_temp, L0_ffn_Wd0, L0_ffn_Wu0, L0_ffn_Wd1, L0_ffn_Wu1, L0_ffn_Wd2, L0_ffn_Wu2, L0_ffn_Wd3, L0_ffn_Wu3)
    return x

_drawn_inputs = setup_inputs


def setup_inputs(seed=0):
    import zlib

    import numpy as np

    out = dict(_drawn_inputs(seed))
    spreads = {'L0_attn_a_norm_weight': (1.0, 0.2),
     'L0_attn_b_ln_w': (1.0, 0.2),
     'L0_attn_b_ln_b': (0.0, 0.1),
     'L0_ffn_bp': (0.0, 0.8)}
    factors = {'L0_ffn_Wd0': 2.801,
     'L0_ffn_Wu0': 2.718,
     'L0_ffn_Wd1': 4.086,
     'L0_ffn_Wu1': 3.996,
     'L0_ffn_Wd2': 6.175,
     'L0_ffn_Wu2': 6.007,
     'L0_ffn_Wd3': 8.0,
     'L0_ffn_Wu3': 8.0}
    for name, (base, spread) in spreads.items():
        noise = np.random.default_rng([zlib.crc32(name.encode()), seed]).standard_normal(out[name].shape)
        drawn = base * np.exp(spread * noise) if base else spread * noise
        out[name] = jnp.asarray(drawn.astype(out[name].dtype))
    for name, factor in factors.items():
        out[name] = (out[name] * factor).astype(out[name].dtype)
    return out
```

```python
from contextlib import ExitStack

import concourse.bass as bass
from concourse import mybir

F32 = mybir.dt.float32
F16 = mybir.dt.float16
ALU = mybir.AluOpType
ACT = mybir.ActivationFunctionType
AX = mybir.AxisListType

P = 128
D = 256
ND = D // P
NHEAD = 16
DH = 64
F = NHEAD * DH
NHALF = 2
HH = NHEAD // NHALF
FH = F // NHALF
NF = F // P
PROJ = 64
RANKS = (1, 2, 4, 8)
NE = len(RANKS)
NR = sum(RANKS)
REST = PROJ + NR + NE
LN_EPS = 1e-5
RMS_EPS = 1e-6
CLAMP_MAX = 4.605170185988092
W_SCALE = 64.0
SM_SCALE = 1.0 / 16.0
NKEY = 3


def token_mixer_stack(nc, x, out, ident, same_head, log_decay, qk, norm_w, o_wT, w_qkvT, w_v, w_outT,
                      ln_wb, w_ffnT, w_p, b_p, b_row, sim, temp, w_up):
    S, T, _ = x.shape
    NB = T // P
    assert S == 4 and x.shape[2] == D and NB % 2 == 0

    ctx = ExitStack()
    with ctx:
        def sb(name, shape, dt=F32):
            return ctx.enter_context(nc.sbuf_tensor(name, shape, dt))

        def sem(name):
            return ctx.enter_context(nc.semaphore(name))

        identity = sb("identity", [P, P])
        ones = sb("ones", [P, P])
        decay = sb("decay", [P, ND])
        qk_in = sb("qk_in", [P, 2, ND])
        qk_prod = sb("qk_prod", [P, ND])
        c_gain = sb("c_gain", [P, ND])
        nw = sb("nw", [P, ND])
        cnw = sb("cnw", [P, ND])
        WO_A = sb("WO_A", [P, ND, D])
        W_HI = sb("W_HI", [P, ND, 3 * F], F16)
        W_LO = sb("W_LO", [P, ND, 3 * F], F16)
        W_OUT = sb("W_OUT", [P, NF, D])
        W_VO = sb("W_VO", [P, ND, D])
        LNWB = sb("LNWB", [P, 2, ND])
        W_FFN = sb("W_FFN", [P, ND, D + REST])
        WP = sb("WP", [PROJ, D])
        BP = sb("BP", [PROJ, 1])
        BROW = sb("BROW", [P, REST])
        SIM = sb("SIM", [PROJ, NE])
        SIM2 = sb("SIM2", [PROJ, NE])
        SIMI = sb("SIMI", [PROJ, NE])
        TEMP = sb("TEMP", [PROJ, 1])
        W_UP = sb("W_UP", [NR, D])
        m_half = sb("m_half", [P, S])
        m_one = sb("m_one", [P, S])
        carry = sb("carry", [P, ND, S])

        X = [sb(f"X{b}", [P, S, D]) for b in range(2)]
        R = [sb(f"R{b}", [P, S, D]) for b in range(2)]
        head_ones = R[0][:, 0, 0:P]
        BPB = R[1][0:PROJ, 0, 0:P]
        X3 = sb("X3", [P, S, D])
        XN = sb("XN", [P, S, D])
        Y = sb("Y", [P, ND, S, P])
        XT = sb("XT", [P, ND, S * P])
        YSQ = XT
        XLT = sb("XLT", [P, ND, S, P])
        XD = sb("XD", [P, ND, NKEY, P])
        XH = [sb(f"XH{b}", [P, ND, S, P], F16) for b in range(2)]
        XL = [sb(f"XL{b}", [P, ND, S, P], F16) for b in range(2)]
        DHI = [sb(f"DHI{b}", [P, ND, NKEY, P], F16) for b in range(2)]
        DLO = [sb(f"DLO{b}", [P, ND, NKEY, P], F16) for b in range(2)]
        Q = [sb(f"Q{h}", [P, S, FH]) for h in range(2)]
        K = [sb(f"K{h}", [P, NKEY, FH]) for h in range(2)]
        V = [sb(f"V{h}", [P, NKEY, FH]) for h in range(2)]
        PD = [sb(f"PD{b}", [P, NKEY, FH]) for b in range(3)]
        PS = sb("PS", [P, NKEY, FH])
        PV = PS
        SC = [sb(f"SC{h}", [P, S, 4, HH]) for h in range(2)]
        SM = [sb(f"SM{h}", [P, S, HH]) for h in range(2)]
        SD = [sb(f"SD{h}", [P, S, 4, HH]) for h in range(2)]
        SE = [sb(f"SE{h}", [P, S, 4, HH]) for h in range(2)]
        SS = [sb(f"SS{h}", [P, S, HH]) for h in range(2)]
        SI = [sb(f"SI{h}", [P, S, HH]) for h in range(2)]
        PR = [sb(f"PR{h}", [P, S, NKEY, HH]) for h in range(2)]
        O = [sb(f"O{h}", [P, S, FH]) for h in range(2)]
        OT = sb("OT", [P, NF, S * P])
        BS = [sb(f"BS{k}", [P, S, 6]) for k in range(4)]
        MV = [sb(f"MV{k}", [P, S, 2]) for k in range(4)]
        VE = [sb(f"VE{k}", [P, S]) for k in range(4)]
        NM = [sb(f"NM{k}", [P, S]) for k in range(4)]
        RS = [sb(f"RS{k}", [P, S]) for k in range(4)]
        NR_ = [sb(f"NR{k}", [P, S]) for k in range(4)]
        MS = sb("MS", [P, S])
        RMS = sb("RMS", [P, S])
        B1 = sb("B1", [P, S])
        B2 = sb("B2", [P, S])
        B3 = sb("B3", [P, S])
        R12 = sb("R12", [P, S])
        NR12 = sb("NR12", [P, S])
        R1P = sb("R1P", [P, S])
        junk = sb("junk", [P, S, PROJ])
        hgT = sb("hgT", [NR, S * P])
        G = []
        for k in range(2):
            G.append({n: sb(f"{n}{k}", s) for n, s in dict(
                rest=[P, S, REST], n2=[P, S], nc=[P, S], ni=[P, S], lg=[P, S, NE],
                m=[P, S], d=[P, S, NE], eq=[P, S, NE], ne=[P, S, 2], cu=[P, S, NE], sel=[P, S, NE], e=[P, S, NE], s2=[P, S, 2], s1=[P, S, 1], si=[P, S, 1],
                ge=[P, S, NE], g=[P, S, NE], hg=[P, S, NR]).items()})

        qkv_ps = [ctx.enter_context(nc.psum_tensor(f"qkv_ps{b}", [P, FH], F32)) for b in range(3)]
        tp = ctx.enter_context(nc.psum_tensor("tp", [P, ND, S * P], F32))
        acc = ctx.enter_context(nc.psum_tensor("acc", [P, S, D], F32))
        small = ctx.enter_context(nc.psum_tensor("small", [P, 512], F32))
        rest_ps = small[:, 0:S * REST].rearrange("p (s r) -> p s r", s=S)
        ssq_ps = small[:, 340:340 + S]

        NQ = NHALF * (NKEY + S + NKEY)
        c_loaded = sem("c_loaded")
        w_staged = sem("w_staged")
        temp_clamped = sem("temp_clamped")
        temp_exp = sem("temp_exp")
        decay_exp = sem("decay_exp")
        halves_set = sem("halves_set")
        qk_multiplied = sem("qk_multiplied")
        gain_summed = sem("gain_summed")
        sim_squared = sem("sim_squared")
        sim_summed = sem("sim_summed")
        sim_norm2 = sem("sim_norm2")
        sim_scale = sem("sim_scale")
        sim_ready = sem("sim_ready")
        router_made = sem("router_made")
        vo_made = sem("vo_made")
        vo_kept = sem("vo_kept")
        w_high = sem("w_high")
        weights_ready = sem("weights_ready")
        x_loaded = [sem(f"x_loaded{b}") for b in range(2)]
        stored = sem("stored")
        dve_step = sem("dve_step")
        pool_step = sem("pool_step")
        ln_var = [sem(f"ln_var{k}") for k in range(4)]
        ln_scale = [sem(f"ln_scale{k}") for k in range(4)]
        ln_rows = [sem(f"ln_rows{k}") for k in range(4)]
        ln_T = [sem(f"ln_T{k}") for k in range(4)]
        scanned = sem("scanned")
        squared = sem("squared")
        projected = sem("projected")
        ms_ready = sem("ms_ready")
        rms_ready = sem("rms_ready")
        x1_ready = sem("x1_ready")
        xT_ready = [sem(f"xT_ready{k}") for k in range(2)]
        rest_done = [sem(f"rest_done{k}") for k in range(2)]
        rest_kept = [sem(f"rest_kept{k}") for k in range(2)]
        n2_ready = [sem(f"n2_ready{k}") for k in range(2)]
        lg_ready = [sem(f"lg_ready{k}") for k in range(2)]
        d_ready = [sem(f"d_ready{k}") for k in range(2)]
        e_ready = [sem(f"e_ready{k}") for k in range(2)]
        hg_ready = [sem(f"hg_ready{k}") for k in range(2)]
        hgT_done = [sem(f"hgT_done{k}") for k in range(2)]
        hgT_kept = [sem(f"hgT_kept{k}") for k in range(2)]
        ffn_done = [sem(f"ffn_done{k}") for k in range(2)]
        ffn_added = [sem(f"ffn_added{k}") for k in range(2)]
        res_scaled = sem("res_scaled")
        xlT_ready = sem("xlT_ready")
        xh_ready = sem("xh_ready")
        xl_ready = sem("xl_ready")
        xd_ready = sem("xd_ready")
        dh_ready = sem("dh_ready")
        dl_ready = sem("dl_ready")
        vo_done = sem("vo_done")
        res_ready = sem("res_ready")
        qkv_done = [sem(f"qkv_done{g}") for g in range(NQ)]
        qkv_kept = [sem(f"qkv_kept{g}") for g in range(NQ)]
        qk_pool = [sem(f"qk_pool{h}") for h in range(2)]
        s_ready = [sem(f"s_ready{h}") for h in range(2)]
        exp_ready = [sem(f"exp_ready{h}") for h in range(2)]
        p_ready = [sem(f"p_ready{h}") for h in range(2)]
        pv_dve = [sem(f"pv_dve{h}") for h in range(2)]
        pv_pool = [sem(f"pv_pool{h}") for h in range(2)]
        oT_done = [sem(f"oT_done{r}") for r in range(4)]
        oT_kept = [sem(f"oT_kept{r}") for r in range(4)]
        out_done = sem("out_done")
        x3_ready = sem("x3_ready")

        stage_qkv = [b.rearrange("p a n -> p (a n)").rearrange("p (c n) -> p c n", c=ND)
                     for b in (Q[0][:, :, :], Q[1][:, :, :], O[1][:, :, :])]
        stage_v = O[0][:, :, :].rearrange("p a n -> p (a n)").rearrange("p (c n) -> p c n", c=NF)
        NLOADS = 16

        def group(g):
            h, k = divmod(g, NQ // 2)
            if k < NKEY:
                return h, "k", k
            if k < NKEY + S:
                return h, "q", k - NKEY
            return h, "v", k - NKEY - S

        def gq(h, i):
            return h * (NQ // 2) + NKEY + i

        def gk(h):
            return h * (NQ // 2) + NKEY - 1

        def gv(h):
            return h * (NQ // 2) + NQ // 2 - 1

        def waiter(eng, at):
            def wait(s, k):
                v = at(k)
                if not isinstance(v, int) or v > 0:
                    eng.wait_ge(s, v)
            return wait

        def run_slots(eng, slot, spread):
            first, last = 2, NB - 3

            def whole(t):
                slot(lambda k: t + k, t, t % 2, t)
            for t in range(-1, first):
                whole(t)
            with eng.Fori(first, last, 2) as i:
                at = {k: eng.snap(i + k) for k in range(spread[0], spread[1] + 2)}
                slot(lambda k: at[k], None, first % 2, i)
                slot(lambda k: at[k + 1], None, (first + 1) % 2, i + 1)
            for t in range(last + 1, NB + 1):
                whole(t)

        def parts(t):
            if t is None:
                return True, True, True, True
            return t + 1 < NB, 0 <= t < NB, 1 <= t <= NB, 1 <= t <= NB

        block = ctx.enter_context(nc.Block())

        @block.sync
        def _(sp):
            loads = [(qk_in[:, :, :], qk), (head_ones, same_head), (decay[:, :], log_decay),
                     (nw[:, :], norm_w), (SIM[:, :], sim), (TEMP[:, :], temp.broadcast_to([PROJ, 1])),
                     (WP[:, :], w_p), (BP[:, :], b_p), (BROW[:, 0:PROJ], b_row.broadcast_to([P, PROJ])),
                     (identity[:, :], ident),
                     (LNWB[:, :, :], ln_wb), (W_UP[:, :], w_up), (WO_A[:, :, :], o_wT),
                     (W_FFN[:, :, 0:D + PROJ + NR], w_ffnT), (W_OUT[:, :, :], w_outT),
                     (stage_v, w_v)]
            assert len(loads) == NLOADS

            def load(n, par):
                sp.dma_start(X[par][:, :, :], x[:, bass.ds(n * P, P), :].rearrange("s t f -> t s f")
                             ).then_inc(x_loaded[par], 16)

            load(0, 0)
            for dst, src in loads:
                sp.dma_start(dst, src).then_inc(c_loaded, 16)
            for c in range(3):
                sp.dma_start(stage_qkv[c], w_qkvT[:, :, c * F:(c + 1) * F]).then_inc(w_staged, 16)

            def slot(at, t, par, n):
                wait = waiter(sp, at)
                if t is None or t + 2 < NB:
                    wait(res_ready, 1)
                    load(n + 2, par)
                if t is None or t >= 1:
                    wait(ffn_added[1], 0)
                    sp.dma_start(out[:, bass.ds((n - 1) * P, P), :].rearrange("s t f -> t s f"),
                                 X3[:, :, :]).then_inc(stored, 16)

            run_slots(sp, slot, (0, 1))
            sp.wait_ge(stored, 16 * NB)

        @block.tensor
        def _(pe):
            def wvo_and_router_weights():
                pe.wait_ge(c_loaded, 16 * NLOADS)
                pe.wait_ge(qk_multiplied, 1)
                pe.matmul(small[:, 0:ND], head_ones, qk_prod[:, :], start=True, stop=True
                          ).then_inc(gain_summed, 1)
                pe.wait_ge(sim_squared, 1)
                pe.matmul(small[0:PROJ, 8:8 + NE], ones[0:PROJ, 0:PROJ], SIM2[:, :], start=True,
                          stop=True).then_inc(sim_summed, 1)
                for c in range(ND):
                    for f in range(NF):
                        mm = pe.matmul(tp[:, c, 0:D], stage_v[:, f, c * P:(c + 1) * P], W_OUT[:, f, :],
                                       start=f == 0, stop=f == NF - 1)
                mm.then_inc(vo_made, 1)
                pe.wait_ge(sim_ready, 1)
                for c in range(ND):
                    pe.matmul(small[:, 16 + NE * c:16 + NE * (c + 1)], WP[:, c * P:(c + 1) * P],
                              SIMI[:, :], start=True, stop=True)
                pe.matmul(small[:, 32:32 + NE], BPB, SIMI[:, :], start=True, stop=True
                          ).then_inc(router_made, 1)
                pe.wait_ge(vo_kept, 1)
                pe.wait_ge(weights_ready, 1)

            def qkv_group(wait, par, g, first):
                h, kind, k = group(g)
                if g >= 3:
                    wait(qkv_kept[g - 3], 1)
                else:
                    last = max(q for q in range(NQ) if q % 3 == g)
                    wait(qkv_kept[last], 0)
                if g == 0:
                    wait(dh_ready, 1)
                    wait(dl_ready, 1)
                if g == NKEY:
                    wait(xh_ready, 1)
                    wait(xl_ready, 1)
                hi, lo, i = (XH[par], XL[par], k) if kind == "q" else (DHI[par], DLO[par], k)
                col = "qkv".index(kind) * F + h * FH
                n = 0
                for c in range(ND):
                    for a, w in ((hi, W_HI), (hi, W_LO), (lo, W_HI)):
                        mm = pe.matmul(qkv_ps[g % 3][:, :], a[:, c, i, :], w[:, c, col:col + FH],
                                       start=n == 0, stop=n == 3 * ND - 1)
                        n += 1
                mm.then_inc(qkv_done[g], 1)

            def transposes(src, done):
                for s in range(S):
                    for c in range(ND):
                        mm = pe.transpose(tp[:, c, s * P:(s + 1) * P], src[:, s, c * P:(c + 1) * P],
                                          identity[:, :])
                mm.then_inc(done, 1)

            def project(wait):
                wait(squared, 2)
                wait(ffn_added[1], -1)
                wait(rest_kept[1], -1)
                for s in range(S):
                    for c in range(ND):
                        pe.matmul(ssq_ps[:, s:s + 1], YSQ[:, c, s * P:(s + 1) * P], ones[:, 0:1],
                                  start=c == 0, stop=c == ND - 1)
                for s in range(S):
                    for c in range(ND):
                        mm = pe.matmul(acc[:, s, :], Y[:, c, s, :], WO_A[:, c, :], start=c == 0,
                                       stop=c == ND - 1)
                mm.then_inc(projected, 1)

            def rest(wait, k, off, do_a=True):
                wait(xT_ready[k], off)
                if k == 0:
                    wait(ms_ready, off)
                elif do_a:
                    wait(rest_kept[0], off + 2)
                for s in range(S):
                    for c in range(ND):
                        mm = pe.matmul(rest_ps[:, s, :], XT[:, c, s * P:(s + 1) * P],
                                       W_FFN[:, c, D:D + REST], start=c == 0, stop=c == ND - 1)
                mm.then_inc(rest_done[k], 1)

            def gate_T(wait, k, off):
                wait(hg_ready[k], off)
                for s in range(S):
                    mm = pe.transpose(tp[0:NR, 0, s * P:(s + 1) * P], G[k]["hg"][:, s, :], identity[:, :])
                mm.then_inc(hgT_done[k], 1)

            def base_and_up(wait, k, off):
                wait(hgT_kept[k], off)
                for s in range(S):
                    for c in range(ND):
                        pe.matmul(acc[:, s, :], XT[:, c, s * P:(s + 1) * P], W_FFN[:, c, 0:D],
                                  start=c == 0, stop=False)
                    mm = pe.matmul(acc[:, s, :], hgT[:, s * P:(s + 1) * P], W_UP[:, :],
                                   start=False, stop=True)
                mm.then_inc(ffn_done[k], 1)

            def o_transposes(wait, r):
                h, part = divmod(r, 2)
                for q in range(2):
                    for i in range(S):
                        c = 2 * part + q
                        mm = pe.transpose(tp[:, q, i * P:(i + 1) * P], O[h][:, i, c * P:(c + 1) * P],
                                          identity[:, :])
                mm.then_inc(oT_done[r], 1)

            wvo_and_router_weights()

            def slot(at, t, par, n):
                wait = waiter(pe, at)
                do_a, do_q, _, do_c = parts(t)

                def groups(a, b):
                    if do_q:
                        for g in range(a, b):
                            qkv_group(wait, par, g, t == 0)

                groups(0, 2)
                if do_a:
                    wait(ln_rows[0], 2)
                    wait(hgT_kept[1], -1)
                    transposes(XN, ln_T[0])
                groups(2, 5)
                if do_a:
                    project(wait)
                if do_c:
                    wait(pv_dve[0], 0)
                    wait(pv_pool[0], 0)
                    if do_a:
                        wait(scanned, 2)
                    o_transposes(wait, 0)
                groups(5, 7)
                if do_c:
                    wait(oT_kept[0], 0)
                    o_transposes(wait, 1)
                if do_a:
                    wait(ln_rows[1], 2)
                    if do_c:
                        wait(oT_kept[1], 0)
                    else:
                        wait(scanned, 2)
                    transposes(XN, ln_T[1])
                groups(7, 9)
                if do_a:
                    rest(wait, 0, 2)
                groups(9, 12)
                if do_a:
                    wait(xT_ready[0], 2)
                    gate_T(wait, 0, 2)
                    wait(x1_ready, 2)
                    base_and_up(wait, 0, 2)
                if do_c:
                    wait(pv_dve[1], 0)
                    wait(pv_pool[1], 0)
                    if do_a:
                        wait(hgT_kept[0], 2)
                    else:
                        wait(oT_kept[1], 0)
                    o_transposes(wait, 2)
                groups(12, 13)
                if do_c:
                    wait(oT_kept[2], 0)
                    o_transposes(wait, 3)
                groups(13, 14)
                if do_a:
                    wait(ln_rows[2], 2)
                    if do_c:
                        wait(oT_kept[3], 0)
                    transposes(XN, ln_T[2])
                if do_c:
                    wait(oT_kept[3], 0)
                    if do_a:
                        wait(ffn_added[0], 2)
                    for s in range(S):
                        for c in range(NF):
                            mm = pe.matmul(acc[:, s, :], OT[:, c, s * P:(s + 1) * P], W_OUT[:, c, :],
                                           start=c == 0, stop=c == NF - 1)
                    mm.then_inc(out_done, 1)
                groups(14, 16)
                if do_a:
                    wait(xlT_ready, 2)
                    if do_c:
                        wait(x3_ready, 0)
                    for c in range(ND):
                        mm = pe.matmul(acc[:, 0, :], XLT[:, c, 0, :], W_VO[:, c, :], start=c == 0,
                                       stop=c == ND - 1)
                    mm.then_inc(vo_done, 1)
                if do_c:
                    wait(ln_rows[3], 0)
                    if do_a:
                        wait(xlT_ready, 2)
                    else:
                        wait(oT_kept[3], 0)
                    transposes(XN, ln_T[3])
                groups(16, 17)
                if do_c:
                    rest(wait, 1, 0, do_a)
                groups(17, 20)
                if do_c:
                    wait(xT_ready[1], 0)
                    gate_T(wait, 1, 0)
                    if do_a:
                        wait(res_ready, 2)
                    base_and_up(wait, 1, 0)

            run_slots(pe, slot, (-1, 2))

        @block.scalar
        def _(act):
            act.wait_ge(c_loaded, 16 * NLOADS)
            act.activation(decay[:, :], decay[:, :], ACT.Exp, scale=-1.0).then_inc(decay_exp, 1)
            act.wait_ge(temp_clamped, 1)
            act.activation(TEMP[:, :], TEMP[:, :], ACT.Exp).then_inc(temp_exp, 1)
            act.wait_ge(w_staged, 48)
            for c in range(3):
                a = act.activation(W_HI[:, :, c * F:(c + 1) * F], stage_qkv[c], ACT.Copy, scale=W_SCALE)
            a.then_inc(w_high, 1)
            act.wait_ge(vo_made, 1)
            act.activation(W_VO[:, :, :], tp[:, :, 0:D], ACT.Copy).then_inc(vo_kept, 1)
            act.wait_ge(weights_ready, 1)

            def rows(src, dst, k):
                for s in range(S):
                    a = act.activation(dst[:, s, :], src[:, s, :], ACT.Identity, scale=RS[k][:, s:s + 1],
                                       bias=NR_[k][:, s:s + 1])
                a.then_inc(ln_rows[k], 1)

            def keep_qkv(wait, g):
                h, kind, k = group(g)
                if g % (NQ // 2) == 0:
                    wait(s_ready[h], 0)
                if kind == "v" and k == 0:
                    wait(pv_dve[h], 0)
                    wait(pv_pool[h], 0)
                wait(qkv_done[g], 1)
                dst = {"q": Q, "k": K, "v": V}[kind][h][:, k, :]
                act.activation(dst, qkv_ps[g % 3][:, :], ACT.Copy, scale=1.0 / W_SCALE
                               ).then_inc(qkv_kept[g], 1)

            def keep_T(k):
                for c in range(ND):
                    a = act.activation(XT[:, c, :], tp[:, c, :], ACT.Copy)
                a.then_inc(xT_ready[k], 1)

            def norms(wait, k, off):
                wait(rest_kept[k], off)
                for s in range(S):
                    a = act.activation(junk[:, s, :], G[k]["rest"][:, s, 0:PROJ], ACT.Square,
                                       accum_out=G[k]["n2"][:, s:s + 1])
                a.then_inc(n2_ready[k], 1)

            def router_exp(wait, k, off):
                wait(d_ready[k], off)
                act.activation(G[k]["e"][:, :, :], G[k]["d"][:, :, :], ACT.Exp).then_inc(e_ready[k], 1)

            def keep_gT(wait, k, off):
                wait(hgT_done[k], off)
                act.activation(hgT[:, :], tp[0:NR, 0, :], ACT.Copy).then_inc(hgT_kept[k], 1)

            def keep_oT(wait, r):
                wait(oT_done[r], 0)
                if r == 0:
                    wait(out_done, -1)
                for q in range(2):
                    a = act.activation(OT[:, 2 * r + q, :], tp[:, q, :], ACT.Copy)
                a.then_inc(oT_kept[r], 1)

            def softmax_exp(wait, h, off):
                wait(s_ready[h], off)
                act.activation(SE[h][:, :, :, :], SD[h][:, :, :, :], ACT.Exp, scale=SM_SCALE
                               ).then_inc(exp_ready[h], 1)

            def slot(at, t, par, n):
                wait = waiter(act, at)
                do_a, do_q, do_u, do_c = parts(t)
                xa = X[1 - par]

                def keeps(a, b):
                    if do_q:
                        for g in range(a, b):
                            keep_qkv(wait, g)

                if do_a:
                    wait(ln_scale[0], 2)
                    wait(ln_T[2], 1)
                    rows(xa, XN, 0)
                keeps(0, 2)
                keeps(2, 5)
                if do_a:
                    wait(scanned, 2)
                    for c in range(ND):
                        a = act.activation(YSQ[:, c, :], Y[:, c, :, :].rearrange("p s t -> p (s t)"),
                                           ACT.Square, scale=c_gain[:, c:c + 1])
                    a.then_inc(squared, 1)
                if do_u:
                    softmax_exp(wait, 1, 0)
                if do_c:
                    keep_oT(wait, 0)
                keeps(5, 7)
                if do_a:
                    wait(ln_scale[1], 2)
                    wait(ln_T[0], 2)
                    rows(xa, XN, 1)
                if do_c:
                    keep_oT(wait, 1)
                if do_a:
                    wait(ln_T[1], 2)
                    keep_T(0)
                keeps(7, 9)
                if do_a:
                    norms(wait, 0, 2)
                keeps(9, 12)
                if do_a:
                    router_exp(wait, 0, 2)
                    keep_gT(wait, 0, 2)
                if do_c:
                    keep_oT(wait, 2)
                keeps(12, 13)
                if do_c:
                    keep_oT(wait, 3)
                keeps(13, 14)
                if do_q:
                    softmax_exp(wait, 0, 1)
                if do_a:
                    wait(ln_scale[2], 2)
                    wait(ln_T[1], 2)
                    for s in range(S):
                        a = act.activation(XN[:, s, :], xa[:, s, :], ACT.Identity,
                                           scale=R12[:, s:s + 1], bias=NR12[:, s:s + 1])
                    a.then_inc(ln_rows[2], 1)
                    wait(x3_ready, 0)
                    for s in range(S):
                        a = act.activation(R[1 - par][:, s, :], xa[:, s, :], ACT.Identity,
                                           scale=R1P[:, s:s + 1], bias=NR_[2][:, s:s + 1])
                    a.then_inc(res_scaled, 1)
                    wait(ln_T[2], 2)
                    for c in range(ND):
                        a = act.activation(XLT[:, c, :, :].rearrange("p s t -> p (s t)"), tp[:, c, :],
                                           ACT.Identity, scale=LNWB[:, 0, c:c + 1],
                                           bias=LNWB[:, 1, c:c + 1])
                    a.then_inc(xlT_ready, 1)
                    wait(xlT_ready, 2)
                    act.activation(XH[1 - par][:, :, :, :], XLT[:, :, :, :], ACT.Copy
                                   ).then_inc(xh_ready, 1)
                    wait(xd_ready, 2)
                    act.activation(DHI[1 - par][:, :, :, :], XD[:, :, :, :], ACT.Copy
                                   ).then_inc(dh_ready, 1)
                keeps(14, 16)
                if do_c:
                    wait(ln_scale[3], 0)
                    rows(X3, XN, 3)
                    wait(ln_T[3], 0)
                    keep_T(1)
                keeps(16, 17)
                if do_c:
                    norms(wait, 1, 0)
                keeps(17, 20)
                if do_c:
                    router_exp(wait, 1, 0)
                    keep_gT(wait, 1, 0)

            run_slots(act, slot, (-1, 2))

        @block.gpsimd
        def _(pool):
            steps = [0]

            def link(ins):
                steps[0] += 1
                ins.then_inc(pool_step, 1)
                pool.wait_ge(pool_step, steps[0])

            def restart():
                pool.sem_clear(pool_step)
                steps[0] = 0

            def settle():
                pool.wait_ge(halves_set, 1)

            pool.memset(m_one[:, :], -1.0)
            for k in range(2):
                pool.memset(G[k]["cu"][:, :, 0:1], 1.0)
            pool.memset(m_half[:, :], -0.5).then_inc(halves_set, 1)
            settle()
            pool.wait_ge(sim_norm2, 1)
            pool.tensor_tensor(SIMI[:, :], SIM2[:, :], m_half[0:PROJ, :], ALU.pow).then_inc(sim_scale, 1)
            pool.wait_ge(weights_ready, 1)

            def row_scale(wait, k, off):
                settle()
                wait(ln_var[k], off)
                link(pool.tensor_tensor(RS[k][:, :], VE[k][:, :], m_half[:, :], ALU.pow))
                pool.tensor_tensor(NR_[k][:, :], NM[k][:, :], RS[k][:, :], ALU.mult
                                   ).then_inc(ln_scale[k], 1)

            def router(wait, k, off):
                g = G[k]
                settle()
                wait(n2_ready[k], off)
                link(pool.tensor_scalar(g["nc"][:, :], g["n2"][:, :], 1e-24, None, ALU.max))
                link(pool.tensor_tensor(g["ni"][:, :], g["nc"][:, :], m_half[:, :], ALU.pow))
                pool.tensor_tensor(g["lg"][:, :, :], g["rest"][:, :, PROJ + NR:REST],
                                   g["ni"][:, :, None].broadcast_to([P, S, NE]), ALU.mult
                                   ).then_inc(lg_ready[k], 1)
                settle()
                wait(d_ready[k], off)
                d, cu, ne = g["d"], g["cu"], g["ne"]
                pool.tensor_scalar(g["eq"][:, :, :], d[:, :, :], 0.0, None, ALU.is_ge)
                pool.tensor_scalar(ne[:, :, :], d[:, :, 1:3], 0.0, None, ALU.is_lt)
                link(pool.tensor_scalar(cu[:, :, 1:2], d[:, :, 0:1], 0.0, None, ALU.is_lt))
                link(pool.tensor_tensor(cu[:, :, 2:3], cu[:, :, 1:2], ne[:, :, 0:1], ALU.mult))
                link(pool.tensor_tensor(cu[:, :, 3:4], cu[:, :, 2:3], ne[:, :, 1:2], ALU.mult))
                link(pool.tensor_tensor(g["sel"][:, :, :], g["eq"][:, :, :], cu[:, :, :], ALU.mult))
                settle()
                wait(e_ready[k], off)
                link(pool.tensor_tensor(g["s2"][:, :, :], g["e"][:, :, 0:2], g["e"][:, :, 2:4], ALU.add))
                link(pool.tensor_tensor(g["s1"][:, :, :], g["s2"][:, :, 0:1], g["s2"][:, :, 1:2], ALU.add))
                link(pool.tensor_tensor(g["si"][:, :, 0], g["s1"][:, :, 0], m_one[:, :], ALU.pow))
                link(pool.tensor_tensor(g["ge"][:, :, :], g["e"][:, :, :], g["sel"][:, :, :], ALU.mult))
                link(pool.tensor_tensor(g["g"][:, :, :], g["ge"][:, :, :],
                                        g["si"][:, :, :].broadcast_to([P, S, NE]), ALU.mult))
                settle()
                wait(hgT_done[k], off - 1)
                lo = 0
                for e, r in enumerate(RANKS):
                    last = pool.tensor_tensor(g["hg"][:, :, lo:lo + r],
                                              g["rest"][:, :, PROJ + lo:PROJ + lo + r],
                                              g["g"][:, :, e:e + 1].broadcast_to([P, S, r]), ALU.mult)
                    lo += r
                last.then_inc(hg_ready[k], 1)

            def qk(wait, h, off):
                settle()
                wait(qkv_kept[gq(h, 3)], off)
                wait(s_ready[1 - h], off - 1 + h)
                wait(pv_pool[1 - h], off - 1 + h)
                pool.tensor_tensor(PS[:, :, :], K[h][:, :, :],
                                   Q[h][:, 3:4, :].broadcast_to([P, NKEY, FH]), ALU.mult
                                   ).then_inc(qk_pool[h], 1)

            def pv(wait, h, off):
                settle()
                wait(p_ready[h], off)
                wait(qkv_kept[gv(h)], off)
                wait(oT_done[2 * h + 1], off - 1)
                for i in (2, 3):
                    link(pool.tensor_tensor(
                        PV[:, :, :].rearrange("p j (g d) -> p j g d", g=HH),
                        V[h][:, :, :].rearrange("p j (g d) -> p j g d", g=HH),
                        PR[h][:, i, :, :, None].broadcast_to([P, NKEY, HH, DH]), ALU.mult))
                    link(pool.tensor_tensor(O[h][:, i, :], PV[:, 0, :], PV[:, 1, :], ALU.add))
                    add = pool.tensor_tensor(O[h][:, i, :], O[h][:, i, :], PV[:, 2, :], ALU.add)
                    if i == 2:
                        link(add)
                add.then_inc(pv_pool[h], 1)

            def slot(at, t, par, n):
                wait = waiter(pool, at)
                do_a, do_q, do_u, do_c = parts(t)
                if do_a:
                    row_scale(wait, 0, 2)
                if do_u:
                    qk(wait, 1, 0)
                if do_a:
                    settle()
                    wait(ms_ready, 2)
                    pool.tensor_tensor(RMS[:, :], MS[:, :], m_half[:, :], ALU.pow
                                       ).then_inc(rms_ready, 1)
                    row_scale(wait, 1, 2)
                if do_u:
                    pv(wait, 1, 0)
                if do_a:
                    router(wait, 0, 2)
                if do_q:
                    qk(wait, 0, 1)
                if do_a:
                    settle()
                    wait(ln_var[2], 2)
                    link(pool.tensor_tensor(RS[2][:, :], VE[2][:, :], m_half[:, :], ALU.pow))
                    link(pool.tensor_tensor(NR_[2][:, :], NM[2][:, :], RS[2][:, :], ALU.mult))
                    link(pool.tensor_scalar(R1P[:, :], RS[2][:, :], 1.0, None, ALU.add))
                    link(pool.tensor_tensor(B1[:, :], MV[2][:, :, 1], RS[2][:, :], ALU.mult))
                    link(pool.tensor_tensor(B2[:, :], B1[:, :], RS[2][:, :], ALU.mult))
                    link(pool.tensor_scalar(B3[:, :], B2[:, :], LN_EPS, None, ALU.add))
                    link(pool.tensor_tensor(B1[:, :], B3[:, :], m_half[:, :], ALU.pow))
                    link(pool.tensor_tensor(R12[:, :], RS[2][:, :], B1[:, :], ALU.mult))
                    pool.tensor_tensor(NR12[:, :], NM[2][:, :], R12[:, :], ALU.mult
                                       ).then_inc(ln_scale[2], 1)
                    settle()
                    wait(xlT_ready, 2)
                    pool.tensor_tensor(XD[:, :, :, :], XLT[:, :, 1:S, :],
                                       XLT[:, :, 0:1, :].broadcast_to([P, ND, NKEY, P]), ALU.subtract
                                       ).then_inc(xd_ready, 1)
                    settle()
                    wait(xh_ready, 2)
                    pool.tensor_tensor(XL[1 - par][:, :, :, :], XLT[:, :, :, :], XH[1 - par][:, :, :, :],
                                       ALU.subtract).then_inc(xl_ready, 1)
                    settle()
                    wait(dh_ready, 2)
                    pool.tensor_tensor(DLO[1 - par][:, :, :, :], XD[:, :, :, :], DHI[1 - par][:, :, :, :],
                                       ALU.subtract).then_inc(dl_ready, 1)
                if do_c:
                    row_scale(wait, 3, 0)
                if do_q:
                    pv(wait, 0, 1)
                if do_c:
                    router(wait, 1, 0)
                restart()

            run_slots(pool, slot, (-1, 2))

        @block.vector
        def _(dve):
            steps = [0]

            def mark(ins):
                steps[0] += 1
                ins.then_inc(dve_step, 1)
                return steps[0]

            def link(ins):
                dve.wait_ge(dve_step, mark(ins))

            def restart():
                dve.wait_ge(dve_step, steps[0])
                dve.sem_clear(dve_step)
                steps[0] = 0

            link(dve.memset(ones[:, :], 1.0))
            mark(dve.memset(carry[:, :, :], 0.0))
            for h in range(2):
                mark(dve.memset(SC[h][:, :, :, :], 0.0))
            mark(dve.memset(BROW[:, PROJ + NR:REST], 0.0))
            mark(dve.memset(BROW[:, PROJ:PROJ + NR], 0.0))
            dve.wait_ge(c_loaded, 16 * NLOADS)
            dve.tensor_scalar(TEMP[:, :], TEMP[:, :], CLAMP_MAX, None, ALU.min).then_inc(temp_clamped, 1)
            dve.tensor_tensor(qk_prod[:, :], qk_in[:, 0, :], qk_in[:, 1, :], ALU.mult
                              ).then_inc(qk_multiplied, 1)
            mark(dve.tensor_scalar(BPB, ones[0:PROJ, :], BP[:, 0:1], None, ALU.mult))
            dve.tensor_tensor(SIM2[:, :], SIM[:, :], SIM[:, :], ALU.mult).then_inc(sim_squared, 1)
            dve.wait_ge(gain_summed, 1)
            dve.wait_ge(sim_summed, 1)
            link(dve.tensor_copy(c_gain[:, :], small[:, 0:ND]))
            link(dve.tensor_tensor(cnw[:, :], c_gain[:, :], nw[:, :], ALU.mult))
            for c in range(ND):
                mark(dve.tensor_scalar(WO_A[:, c, :], WO_A[:, c, :], cnw[:, c:c + 1], None, ALU.mult))
            dve.tensor_scalar(SIM2[:, :], small[0:PROJ, 8:8 + NE], 1e-24, None, ALU.max
                              ).then_inc(sim_norm2, 1)
            dve.wait_ge(decay_exp, 1)
            link(dve.tensor_scalar(decay[:, :], decay[:, :], 1.0, None, ALU.add))
            link(dve.reciprocal(decay[:, :], decay[:, :]))
            dve.wait_ge(sim_scale, 1)
            link(dve.tensor_tensor(SIMI[:, :], SIM[:, :], SIMI[:, :], ALU.mult))
            dve.wait_ge(temp_exp, 1)
            dve.tensor_scalar(SIMI[:, :], SIMI[:, :], TEMP[:, 0:1], None, ALU.mult).then_inc(sim_ready, 1)
            dve.wait_ge(router_made, 1)
            for c in range(ND):
                mark(dve.tensor_copy(W_FFN[:, c, D + PROJ + NR:D + REST],
                                     small[:, 16 + NE * c:16 + NE * (c + 1)]))
            link(dve.tensor_copy(BROW[:, PROJ + NR:REST], small[:, 32:32 + NE]))
            dve.wait_ge(w_high, 1)
            for c in range(3):
                a = dve.scalar_tensor_tensor(W_LO[:, :, c * F:(c + 1) * F], stage_qkv[c], W_SCALE,
                                             W_HI[:, :, c * F:(c + 1) * F], ALU.mult, ALU.subtract)
            a.then_inc(weights_ready, 1)
            dve.wait_ge(weights_ready, 1)
            restart()

            def statistics(src, k, eps):
                for s in range(S):
                    last = mark(dve.bn_stats(BS[k][:, s, :], src[:, s, :]))
                dve.wait_ge(dve_step, last)
                for s in range(S):
                    last = mark(dve.bn_aggr(MV[k][:, s, :], BS[k][:, s, :]))
                dve.wait_ge(dve_step, last)
                mark(dve.tensor_scalar(NM[k][:, :], MV[k][:, :, 0], -1.0, None, ALU.mult))
                dve.tensor_scalar(VE[k][:, :], MV[k][:, :, 1], eps, None, ALU.add
                                  ).then_inc(ln_var[k], 1)

            def scan(wait):
                wait(ln_T[0], 2)
                wait(projected, 1)
                wait(scanned, 1)
                for s in range(S):
                    for c in range(ND):
                        a = dve.tensor_tensor_scan(Y[:, c, s, :], decay[:, c:c + 1].broadcast_to([P, P]),
                                                   tp[:, c, s * P:(s + 1) * P], carry[:, c, s:s + 1],
                                                   ALU.mult, ALU.add)
                dve.wait_ge(dve_step, mark(a))
                dve.tensor_copy(carry[:, :, :], Y[:, :, :, P - 1]).then_inc(scanned, 1)

            def keep_rest(wait, k, off):
                wait(rest_done[k], off)
                dve.tensor_tensor(G[k]["rest"][:, :, :], rest_ps[:, :, :],
                                  BROW[:, None, :].broadcast_to([P, S, REST]), ALU.add
                                  ).then_inc(rest_kept[k], 1)

            def maximum(wait, k, off):
                wait(lg_ready[k], off)
                link(dve.tensor_reduce(G[k]["m"][:, :], G[k]["lg"][:, :, :], AX.X, ALU.max))
                dve.tensor_tensor(G[k]["d"][:, :, :], G[k]["lg"][:, :, :],
                                  G[k]["m"][:, :, None].broadcast_to([P, S, NE]), ALU.subtract
                                  ).then_inc(d_ready[k], 1)

            def product(wait, h, off, i):
                wait(qkv_kept[gq(h, i)], off)
                return mark(dve.tensor_tensor(
                    PD[i][:, :, :], K[h][:, :, :], Q[h][:, i:i + 1, :].broadcast_to([P, NKEY, FH]),
                    ALU.mult))

            def total(h, i, src):
                return mark(dve.tensor_reduce(SC[h][:, i, 1:4, :], src[:, :, :].rearrange(
                    "p j (g d) -> p j g d", g=HH), AX.X, ALU.add))

            def qk_first(wait, h, off):
                wait(qkv_kept[gk(h)], off)
                wait(pv_dve[1 - h], off - 1 + h)
                made = [product(wait, h, off, i) for i in range(2)]
                dve.wait_ge(dve_step, made[0])
                total(h, 0, PD[0])
                made.append(product(wait, h, off, 2))
                return made

            def qk_rest(wait, h, off, made):
                dve.wait_ge(dve_step, made[1])
                total(h, 1, PD[1])
                dve.wait_ge(dve_step, made[2])
                total(h, 2, PD[2])
                wait(qk_pool[h], off)
                last = total(h, 3, PS)
                dve.wait_ge(dve_step, last)
                link(dve.tensor_reduce(SM[h][:, :, :], SC[h][:, :, :, :].rearrange("p i j g -> p i g j"),
                                       AX.X, ALU.max))
                dve.tensor_tensor(SD[h][:, :, :, :], SC[h][:, :, :, :],
                                  SM[h][:, :, None, :].broadcast_to([P, S, 4, HH]), ALU.subtract
                                  ).then_inc(s_ready[h], 1)

            def probabilities(wait, h, off):
                wait(exp_ready[h], off)
                link(dve.tensor_reduce(SS[h][:, :, :], SE[h][:, :, :, :].rearrange("p i j g -> p i g j"),
                                       AX.X, ALU.add))
                link(dve.reciprocal(SI[h][:, :, :], SS[h][:, :, :]))
                dve.tensor_tensor(PR[h][:, :, :, :], SE[h][:, :, 1:4, :],
                                  SI[h][:, :, None, :].broadcast_to([P, S, NKEY, HH]), ALU.mult
                                  ).then_inc(p_ready[h], 1)

            def pv(wait, h, off):
                wait(p_ready[h], off)
                wait(qkv_kept[gv(h)], off)
                wait(oT_done[2 * h + 1], off - 1)
                made = [mark(dve.tensor_tensor(
                    PD[i][:, :, :].rearrange("p j (g d) -> p j g d", g=HH),
                    V[h][:, :, :].rearrange("p j (g d) -> p j g d", g=HH),
                    PR[h][:, i, :, :, None].broadcast_to([P, NKEY, HH, DH]), ALU.mult))
                    for i in range(2)]
                half = []
                for i in range(2):
                    dve.wait_ge(dve_step, made[i])
                    half.append(mark(dve.tensor_tensor(PD[i][:, 0, :], PD[i][:, 0, :], PD[i][:, 1, :],
                                                       ALU.add)))
                for i in range(2):
                    dve.wait_ge(dve_step, half[i])
                    a = dve.tensor_tensor(O[h][:, i, :], PD[i][:, 0, :], PD[i][:, 2, :], ALU.add)
                    if i == 0:
                        mark(a)
                a.then_inc(pv_dve[h], 1)

            def slot(at, t, par, n):
                wait = waiter(dve, at)
                do_a, do_q, do_u, do_c = parts(t)
                xa = X[1 - par]
                if do_a:
                    dve.wait_ge(x_loaded[1 - par], n * 8 + 8 * (2 + par))
                    statistics(xa, 0, LN_EPS)
                if do_u:
                    made = qk_first(wait, 1, 0)
                if do_a:
                    scan(wait)
                if do_u:
                    qk_rest(wait, 1, 0, made)
                if do_a:
                    wait(projected, 2)
                    dve.tensor_scalar(MS[:, :], ssq_ps, 1.0 / D, RMS_EPS, ALU.mult, ALU.add
                                      ).then_inc(ms_ready, 1)
                if do_u:
                    probabilities(wait, 1, 0)
                    pv(wait, 1, 0)
                if do_a:
                    wait(rms_ready, 2)
                    for s in range(S):
                        a = dve.scalar_tensor_tensor(xa[:, s, :], acc[:, s, :], RMS[:, s:s + 1],
                                                     xa[:, s, :], ALU.mult, ALU.add)
                    a.then_inc(x1_ready, 1)
                    wait(x1_ready, 2)
                    statistics(xa, 1, LN_EPS)
                    keep_rest(wait, 0, 2)
                if do_q:
                    made = qk_first(wait, 0, 1)
                if do_a:
                    maximum(wait, 0, 2)
                if do_q:
                    qk_rest(wait, 0, 1, made)
                if do_a:
                    wait(ffn_done[0], 2)
                    dve.tensor_tensor(xa[:, :, :], xa[:, :, :], acc[:, :, :], ALU.add
                                      ).then_inc(ffn_added[0], 1)
                    wait(ffn_added[0], 2)
                    statistics(xa, 2, LN_EPS)
                if do_q:
                    probabilities(wait, 0, 1)
                if do_c:
                    wait(out_done, 0)
                    if n - 1 > 0 if t is not None else True:
                        dve.wait_ge(stored, (n - 1) * 16)
                    dve.tensor_tensor(X3[:, :, :], acc[:, :, :], R[1 - par][:, :, :], ALU.add
                                      ).then_inc(x3_ready, 1)
                    wait(x3_ready, 0)
                    statistics(X3, 3, LN_EPS)
                if do_a:
                    wait(vo_done, 2)
                    wait(res_scaled, 2)
                    dve.tensor_tensor(R[1 - par][:, :, :], R[1 - par][:, :, :],
                                      acc[:, 0:1, :].broadcast_to([P, S, D]), ALU.add
                                      ).then_inc(res_ready, 1)
                if do_q:
                    pv(wait, 0, 1)
                if do_c:
                    keep_rest(wait, 1, 0)
                    maximum(wait, 1, 0)
                    wait(ffn_done[1], 0)
                    dve.tensor_tensor(X3[:, :, :], X3[:, :, :], acc[:, :, :], ALU.add
                                      ).then_inc(ffn_added[1], 1)
                restart()

            run_slots(dve, slot, (-1, 2))


_IN = ["x", "ident", "same_head", "log_decay", "qk", "norm_w", "o_wT", "w_qkvT", "w_v", "w_outT", "ln_wb",
       "w_ffnT", "w_p", "b_p", "b_row", "sim", "temp", "w_up"]


def kernel(**inputs):
    import numpy as np
    import concourse.bacc as bacc
    from concourse.bass_utils import run_bass_kernel_spmd

    a = {k.replace("L0_", ""): np.asarray(v) for k, v in inputs.items()}

    def columns(m):
        return m.reshape(-1, P, m.shape[-1]).transpose(1, 0, 2)

    def features(v):
        return v.reshape(-1, P).T

    w = a["attn_b_w_qkv"].reshape(NHEAD, 3, DH, D)
    parts = [w[:, k].reshape(F, D) for k in range(3)]
    dh = D // NHEAD
    arrays = {
        "x": a["attn_a_x"],
        "ident": np.eye(P, dtype=np.float32),
        "same_head": np.kron(np.eye(P // dh, dtype=np.float32), np.ones((dh, dh), np.float32)),
        "log_decay": features(np.repeat(a["attn_a_log_decay"], dh)),
        "qk": np.stack([features(a["attn_a_q"]), features(a["attn_a_k"])], 1),
        "norm_w": features(a["attn_a_norm_weight"]),
        "o_wT": columns(a["attn_a_o_w"].T),
        "w_qkvT": columns(np.concatenate(parts, 0).T),
        "w_v": columns(parts[2]),
        "w_outT": columns(a["attn_b_w_out"].T),
        "ln_wb": np.stack([features(a["attn_b_ln_w"]), features(a["attn_b_ln_b"])], 1),
        "w_ffnT": columns(np.concatenate([a["ffn_W"], a["ffn_Wp"]] + [a[f"ffn_Wd{e}"] for e in range(NE)]).T),
        "w_p": a["ffn_Wp"],
        "b_p": a["ffn_bp"][:, None],
        "b_row": a["ffn_bp"][None, :],
        "sim": a["ffn_sim"],
        "temp": a["ffn_temp"][None, :],
        "w_up": np.concatenate([a[f"ffn_Wu{e}"].T for e in range(NE)]),
    }
    arrays = {k: np.ascontiguousarray(v) for k, v in arrays.items()}

    nc = bacc.Bacc("TRN2", target_bir_lowering=False, num_devices=1)
    args = [nc.dram_tensor(f"in_{k}", arrays[k].shape, mybir.dt.from_np(arrays[k].dtype),
                           kind="ExternalInput").ap() for k in _IN]
    out = nc.dram_tensor("out_x", arrays["x"].shape, F32, kind="ExternalOutput").ap()
    token_mixer_stack(nc, args[0], out, *args[1:])
    r = run_bass_kernel_spmd(nc, [{f"in_{k}": arrays[k] for k in _IN}], core_ids=[0])
    return r.results[0]["out_x"]
```

```python
from contextlib import ExitStack

import concourse.bass as bass
from concourse import mybir

F32 = mybir.dt.float32
F16 = mybir.dt.float16
ALU = mybir.AluOpType
ACT = mybir.ActivationFunctionType
AX = mybir.AxisListType

P = 128
D = 256
ND = D // P
NHEAD = 16
DH = 64
F = NHEAD * DH
NHALF = 2
HH = NHEAD // NHALF
FH = F // NHALF
NF = F // P
PROJ = 64
RANKS = (1, 2, 4, 8)
NE = len(RANKS)
NR = sum(RANKS)
REST = PROJ + NR + NE
LN_EPS = 1e-5
RMS_EPS = 1e-6
CLAMP_MAX = 4.605170185988092
W_SCALE = 64.0
O_SCALE = 8.0
UP = 32
SM_SCALE = 1.0 / 16.0
NKEY = 3


def token_mixer_stack(nc, x, out, ident, same_head, log_decay, qk, norm_w, o_wT, w_qkvT, w_v, w_outT,
                      ln_wb, w_ffnT, w_p, b_p, b_row, sim, temp, w_up):
    S, T, _ = x.shape
    NB = T // P
    assert S == 4 and x.shape[2] == D and NB % 2 == 0

    ctx = ExitStack()
    with ctx:
        def sb(name, shape, dt=F32):
            return ctx.enter_context(nc.sbuf_tensor(name, shape, dt))

        def sem(name):
            return ctx.enter_context(nc.semaphore(name))

        identity = sb("identity", [P, P])
        ones = sb("ones", [P, P])
        decay = sb("decay", [P, ND])
        qk_in = sb("qk_in", [P, 2, ND])
        qk_prod = sb("qk_prod", [P, ND])
        c_gain = sb("c_gain", [P, ND])
        nw = sb("nw", [P, ND])
        cnw = sb("cnw", [P, ND])
        WO_A = sb("WO_A", [P, ND, D])
        W_HI = sb("W_HI", [P, ND, 3 * F], F16)
        W_LO = sb("W_LO", [P, ND, 3 * F], F16)
        W_OUT_HI = sb("W_OUT_HI", [P, NF, D], F16)
        W_OUT_LO = sb("W_OUT_LO", [P, NF, D], F16)
        W_VO = sb("W_VO", [P, ND, D])
        LNWB = sb("LNWB", [P, 2, ND])
        W_FFN = sb("W_FFN", [P, ND, D + REST])
        WP = sb("WP", [PROJ, D])
        BP = sb("BP", [PROJ, 1])
        BROW = sb("BROW", [P, REST])
        SIM = sb("SIM", [PROJ, NE])
        SIM2 = sb("SIM2", [PROJ, NE])
        SIMI = sb("SIMI", [PROJ, NE])
        TEMP = sb("TEMP", [PROJ, 1])
        W_UP = sb("W_UP", [3 * UP, D], F16)
        identity16 = sb("identity16", [P, P], F16)
        m_half = sb("m_half", [P, S])
        m_one = sb("m_one", [P, S])
        carry = sb("carry", [P, ND, S])

        X = [sb(f"X{b}", [P, S, D]) for b in range(2)]
        R = [sb(f"R{b}", [P, S, D]) for b in range(2)]
        head_ones = R[0][:, 0, 0:P]
        BPB = R[1][0:PROJ, 0, 0:P]
        up_stage = R[1][0:3 * UP, 1, :]
        X3 = sb("X3", [P, S, D])
        XN = sb("XN", [P, S, D])
        YSQ = XN[:, :, :].rearrange("p s d -> p (s d)").rearrange("p (c n) -> p c n", c=ND)
        Y = sb("Y", [P, ND, S, P])
        XT0 = sb("XT0", [P, ND, S * P])
        XLT = sb("XLT", [P, ND, S, P])
        XD = sb("XD", [P, ND, NKEY, P])
        XH = [sb(f"XH{b}", [P, ND, S, P], F16) for b in range(2)]
        XL = [sb(f"XL{b}", [P, ND, S, P], F16) for b in range(2)]
        DHI = [sb(f"DHI{b}", [P, ND, NKEY, P], F16) for b in range(2)]
        DLO = [sb(f"DLO{b}", [P, ND, NKEY, P], F16) for b in range(2)]
        Q = [sb(f"Q{h}", [P, S, FH]) for h in range(2)]
        K = [sb(f"K{h}", [P, NKEY, FH]) for h in range(2)]
        V = [sb(f"V{h}", [P, NKEY, FH]) for h in range(2)]
        PD = [sb(f"PD{b}", [P, NKEY, FH]) for b in range(3)]
        PS = sb("PS", [P, NKEY, FH])
        PV = PS
        SC = [sb(f"SC{h}", [P, S, 4, HH]) for h in range(2)]
        SM = [sb(f"SM{h}", [P, S, HH]) for h in range(2)]
        SD = [sb(f"SD{h}", [P, S, 4, HH]) for h in range(2)]
        SE = [sb(f"SE{h}", [P, S, 4, HH]) for h in range(2)]
        SS = [sb(f"SS{h}", [P, S, HH]) for h in range(2)]
        SI = [sb(f"SI{h}", [P, S, HH]) for h in range(2)]
        PR = [sb(f"PR{h}", [P, S, NKEY, HH]) for h in range(2)]
        O = [sb(f"O{h}", [P, S, FH]) for h in range(2)]
        OT_HI = sb("OT_HI", [P, NF, S * P], F16)
        OT_LO = sb("OT_LO", [P, NF, S * P], F16)
        XN3 = O[1][:, 0:2, :].rearrange("p a n -> p (a n)").rearrange("p (s d) -> p s d", s=S)
        XT = [XT0[:, :, :], O[1][:, 2:4, :]]
        BS = [sb(f"BS{k}", [P, S, 6]) for k in range(4)]
        MV = [sb(f"MV{k}", [P, S, 2]) for k in range(4)]
        VE = [sb(f"VE{k}", [P, S]) for k in range(4)]
        NM = [sb(f"NM{k}", [P, S]) for k in range(4)]
        RS = [sb(f"RS{k}", [P, S]) for k in range(4)]
        NR_ = [sb(f"NR{k}", [P, S]) for k in range(4)]
        MS = sb("MS", [P, S])
        RMS = sb("RMS", [P, S])
        B1 = sb("B1", [P, S])
        B2 = sb("B2", [P, S])
        B3 = sb("B3", [P, S])
        R12 = sb("R12", [P, S])
        NR12 = sb("NR12", [P, S])
        R1P = sb("R1P", [P, S])
        junk = [sb(f"junk{k}", [P, S, PROJ], F16) for k in range(2)]
        hgT = sb("hgT", [3 * UP, S * P], F16)
        hg3 = [sb(f"hg3_{k}", [P, S, 3, UP], F16) for k in range(2)]
        G = []
        for k in range(2):
            G.append({n: sb(f"{n}{k}", s) for n, s in dict(
                rest=[P, S, REST], n2=[P, S], nc=[P, S], ni=[P, S], lg=[P, S, NE],
                m=[P, S], d=[P, S, NE], eq=[P, S, NE], ne=[P, S, 2], cu=[P, S, NE], sel=[P, S, NE], e=[P, S, NE], s2=[P, S, 2], s1=[P, S, 1], si=[P, S, 1],
                ge=[P, S, NE], g=[P, S, NE], hg=[P, S, NR]).items()})

        qkv_ps = [ctx.enter_context(nc.psum_tensor(f"qkv_ps{b}", [P, FH], F32)) for b in range(3)]
        tp = ctx.enter_context(nc.psum_tensor("tp", [P, ND, S * P], F32))
        acc = ctx.enter_context(nc.psum_tensor("acc", [P, S, D], F32))
        small = ctx.enter_context(nc.psum_tensor("small", [P, 512], F32))
        rest_ps = small[:, 0:S * REST].rearrange("p (s r) -> p s r", s=S)
        ssq_ps = small[:, 340:340 + S]

        NQ = NHALF * (NKEY + S + NKEY)
        head_loaded = sem("head_loaded")
        ffn_loaded = sem("ffn_loaded")
        out_loaded = sem("out_loaded")
        head_ready = sem("head_ready")
        ffn_ready = sem("ffn_ready")
        w_staged = sem("w_staged")
        temp_clamped = sem("temp_clamped")
        temp_exp = sem("temp_exp")
        decay_exp = sem("decay_exp")
        halves_set = sem("halves_set")
        qk_multiplied = sem("qk_multiplied")
        gain_summed = sem("gain_summed")
        sim_squared = sem("sim_squared")
        sim_summed = sem("sim_summed")
        sim_norm2 = sem("sim_norm2")
        sim_scale = sem("sim_scale")
        sim_ready = sem("sim_ready")
        router_made = sem("router_made")
        vo_made = sem("vo_made")
        vo_kept = sem("vo_kept")
        w_high = sem("w_high")
        weights_ready = sem("weights_ready")
        x_loaded = [sem(f"x_loaded{b}") for b in range(2)]
        base_done = [sem(f"base_done{k}") for k in range(2)]
        stored = sem("stored")
        dve_step = sem("dve_step")
        pool_step = sem("pool_step")
        ln_var = [sem(f"ln_var{k}") for k in range(4)]
        ln_scale = [sem(f"ln_scale{k}") for k in range(4)]
        ln_rows = [sem(f"ln_rows{k}") for k in range(4)]
        ln_T = [sem(f"ln_T{k}") for k in range(4)]
        scanned = sem("scanned")
        squared = sem("squared")
        squares_summed = sem("squares_summed")
        projected = sem("projected")
        ms_ready = sem("ms_ready")
        rms_ready = sem("rms_ready")
        x1_ready = sem("x1_ready")
        xT_ready = [sem(f"xT_ready{k}") for k in range(2)]
        rest_done = [sem(f"rest_done{k}") for k in range(2)]
        rest_kept = [sem(f"rest_kept{k}") for k in range(2)]
        n2_ready = [sem(f"n2_ready{k}") for k in range(2)]
        lg_ready = [sem(f"lg_ready{k}") for k in range(2)]
        d_ready = [sem(f"d_ready{k}") for k in range(2)]
        e_ready = [sem(f"e_ready{k}") for k in range(2)]
        hg_ready = [sem(f"hg_ready{k}") for k in range(2)]
        hgT_done = [sem(f"hgT_done{k}") for k in range(2)]
        hgT_kept = [sem(f"hgT_kept{k}") for k in range(2)]
        ffn_done = [sem(f"ffn_done{k}") for k in range(2)]
        ffn_added = [sem(f"ffn_added{k}") for k in range(2)]
        res_scaled = sem("res_scaled")
        xlT_ready = sem("xlT_ready")
        xh_ready = sem("xh_ready")
        xl_ready = sem("xl_ready")
        xd_ready = sem("xd_ready")
        dh_ready = sem("dh_ready")
        dl_ready = sem("dl_ready")
        vo_done = sem("vo_done")
        res_ready = sem("res_ready")
        qkv_done = [sem(f"qkv_done{g}") for g in range(NQ)]
        qkv_kept = [sem(f"qkv_kept{g}") for g in range(NQ)]
        qk_pool = [sem(f"qk_pool{h}") for h in range(2)]
        s_ready = [sem(f"s_ready{h}") for h in range(2)]
        exp_ready = [sem(f"exp_ready{h}") for h in range(2)]
        p_ready = [sem(f"p_ready{h}") for h in range(2)]
        pv_dve = [sem(f"pv_dve{h}") for h in range(2)]
        pv_pool = [sem(f"pv_pool{h}") for h in range(2)]
        oT_done = [sem(f"oT_done{r}") for r in range(4)]
        oT_high = [sem(f"oT_high{r}") for r in range(4)]
        oT_kept = [sem(f"oT_kept{r}") for r in range(4)]
        out_done = sem("out_done")
        x3_ready = sem("x3_ready")

        N_LOADS = (6, 3, 10)
        stage_qkv = [b.rearrange("p a n -> p (a n)").rearrange("p (c n) -> p c n", c=ND)
                     for b in (Q[0][:, :, :], Q[1][:, :, :], O[1][:, :, :])]
        stage_v = O[0][:, :, :].rearrange("p a n -> p (a n)").rearrange("p (c n) -> p c n", c=NF)
        stage_out = [b.rearrange("p a n -> p (a n)")[:, 0:m * D].rearrange("p (c n) -> p c n", c=m)
                     for b, m in ((V[0][:, :, :], 6), (V[1][:, :, :], NF - 6))]

        def group(g):
            h, k = divmod(g, NQ // 2)
            if k < NKEY:
                return h, "k", k
            if k < NKEY + S:
                return h, "q", k - NKEY
            return h, "v", k - NKEY - S

        def gq(h, i):
            return h * (NQ // 2) + NKEY + i

        def gk(h):
            return h * (NQ // 2) + NKEY - 1

        def gv(h):
            return h * (NQ // 2) + NQ // 2 - 1

        HEAD, TAIL, MIX, PROJ_OUT, LAST = 3, 2, 1, 0, -1
        FIRST_SLOT, LAST_SLOT = -2, NB + 1

        def waiter(eng, t, at):
            def wait(s, k):
                if t is None:
                    eng.wait_ge(s, at[k])
                elif t + k > 0:
                    eng.wait_ge(s, min(t + k, NB))

            def wait_ends(s, k):
                if t is not None:
                    wait(s, k)
            return wait, wait_ends

        def stages(t):
            if t is None:
                return (True,) * 5
            return tuple(0 <= t + d < NB for d in (2, 1, 0, -1, -2))

        def run_slots(eng, slot, spread, before_first=None, before_second=None):
            first, end = 3, NB - 3
            for t in range(FIRST_SLOT, first):
                if t == FIRST_SLOT and before_first:
                    before_first()
                if t == FIRST_SLOT + 1 and before_second:
                    before_second()
                slot(t, None, t % 2, t)
            with eng.Fori(first, end - 1, 2) as i:
                at = {k: eng.snap(i + k) for k in range(spread[0], spread[1] + 2)}
                slot(None, at, first % 2, i)
                slot(None, {k: at[k + 1] for k in range(spread[0], spread[1] + 1)}, (first + 1) % 2, i + 1)
            for t in range(end, LAST_SLOT + 1):
                slot(t, None, t % 2, t)

        block = ctx.enter_context(nc.Block())

        @block.sync
        def _(sp):
            head_loads = [(qk_in[:, :, :], qk), (head_ones, same_head), (decay[:, :], log_decay),
                          (nw[:, :], norm_w), (identity[:, :], ident), (WO_A[:, :, :], o_wT)]
            out_loads = [(stage_v, w_v), (stage_out[0], w_outT[:, 0:6, :]), (stage_out[1], w_outT[:, 6:NF, :])]
            ffn_loads = [(SIM[:, :], sim), (TEMP[:, :], temp.broadcast_to([PROJ, 1])), (WP[:, :], w_p),
                         (BP[:, :], b_p), (BROW[:, 0:PROJ], b_row.broadcast_to([P, PROJ])),
                         (W_FFN[:, :, 0:D + PROJ + NR], w_ffnT), (LNWB[:, :, :], ln_wb)] + [
                             (up_stage[UP * i:UP * i + NR, :], w_up) for i in range(3)]
            assert (len(head_loads), len(out_loads), len(ffn_loads)) == N_LOADS

            def load(n, par):
                sp.dma_start(X[par][:, :, :], x[:, bass.ds(n * P, P), :].rearrange("s t f -> t s f")
                             ).then_inc(x_loaded[par], 16)

            load(0, 0)
            for loads, done in ((head_loads, head_loaded), (ffn_loads, ffn_loaded), (out_loads, out_loaded)):
                for dst, src in loads:
                    sp.dma_start(dst, src).then_inc(done, 16)
            for c in range(3):
                sp.dma_start(stage_qkv[c], w_qkvT[:, :, c * F:(c + 1) * F]).then_inc(w_staged, 16)

            def slot(t, at, par, n):
                wait, _ = waiter(sp, t, at)
                head, _, _, _, last = stages(t)
                if head and (t is None or t > FIRST_SLOT):
                    wait(res_ready, MIX)
                    load(n + 2, par)
                if last:
                    wait(ffn_added[1], LAST)
                    sp.dma_start(out[:, bass.ds((n - 2) * P, P), :].rearrange("s t f -> t s f"),
                                 X3[:, :, :]).then_inc(stored, 16)

            run_slots(sp, slot, (LAST, MIX))
            sp.wait_ge(stored, 16 * NB)

        @block.tensor
        def _(pe):
            def gains():
                pe.wait_ge(head_loaded, 16 * N_LOADS[0])
                pe.wait_ge(qk_multiplied, 1)
                pe.matmul(small[:, 0:ND], head_ones, qk_prod[:, :], start=True, stop=True
                          ).then_inc(gain_summed, 1)
                pe.wait_ge(head_ready, 1)

            def router_weights():
                pe.wait_ge(ffn_loaded, 16 * N_LOADS[2])
                pe.wait_ge(sim_squared, 1)
                pe.wait_ge(ms_ready, 1)
                pe.matmul(small[0:PROJ, 8:8 + NE], ones[0:PROJ, 0:PROJ], SIM2[:, :], start=True,
                          stop=True).then_inc(sim_summed, 1)
                pe.wait_ge(out_loaded, 16 * N_LOADS[1])
                pe.wait_ge(scanned, 1)
                for c in range(ND):
                    for f in range(NF):
                        w = stage_out[0][:, f, :] if f < 6 else stage_out[1][:, f - 6, :]
                        mm = pe.matmul(tp[:, c, 0:D], stage_v[:, f, c * P:(c + 1) * P], w,
                                       start=f == 0, stop=f == NF - 1)
                mm.then_inc(vo_made, 1)
                pe.wait_ge(sim_ready, 1)
                for c in range(ND):
                    pe.matmul(small[:, 16 + NE * c:16 + NE * (c + 1)], WP[:, c * P:(c + 1) * P],
                              SIMI[:, :], start=True, stop=True)
                pe.matmul(small[:, 32:32 + NE], BPB, SIMI[:, :], start=True, stop=True
                          ).then_inc(router_made, 1)
                pe.wait_ge(vo_kept, 1)
                pe.wait_ge(ffn_ready, 1)

            def qkv_group(wait, par, g):
                h, kind, k = group(g)
                if g >= 3:
                    wait(qkv_kept[g - 3], MIX)
                else:
                    wait(qkv_kept[max(q for q in range(NQ) if q % 3 == g)], MIX - 1)
                if g == 0:
                    wait(dh_ready, MIX)
                    wait(dl_ready, MIX)
                if g == NKEY:
                    wait(xh_ready, MIX)
                    wait(xl_ready, MIX)
                hi, lo, i = (XH[par], XL[par], k) if kind == "q" else (DHI[par], DLO[par], k)
                col = "qkv".index(kind) * F + h * FH
                n = 0
                for c in range(ND):
                    for a, w in ((hi, W_HI), (hi, W_LO), (lo, W_HI)):
                        mm = pe.matmul(qkv_ps[g % 3][:, :], a[:, c, i, :], w[:, c, col:col + FH],
                                       start=n == 0, stop=n == 3 * ND - 1)
                        n += 1
                mm.then_inc(qkv_done[g], 1)

            def transposes(src, done):
                for s in range(S):
                    for c in range(ND):
                        mm = pe.transpose(tp[:, c, s * P:(s + 1) * P], src[:, s, c * P:(c + 1) * P],
                                          identity[:, :])
                mm.then_inc(done, 1)

            def project(wait):
                wait(squares_summed, HEAD)
                for s in range(S):
                    pe.matmul(ssq_ps[:, s:s + 1], YSQ[:, 0, s * P:(s + 1) * P], ones[:, 0:1],
                              start=True, stop=True)
                for s in range(S):
                    for c in range(ND):
                        mm = pe.matmul(acc[:, s, :], Y[:, c, s, :], WO_A[:, c, :], start=c == 0,
                                       stop=c == ND - 1)
                mm.then_inc(projected, 1)

            def rest(wait, k, off):
                wait(xT_ready[k], off)
                for s in range(S):
                    for c in range(ND):
                        mm = pe.matmul(rest_ps[:, s, :], XT[k][:, c, s * P:(s + 1) * P],
                                       W_FFN[:, c, D:D + REST], start=c == 0, stop=c == ND - 1)
                mm.then_inc(rest_done[k], 1)

            def gate_T(wait, k, off):
                wait(hg_ready[k], off)
                for s in range(S):
                    mm = pe.matmul(tp[0:3 * UP, 0, s * P:(s + 1) * P],
                                   hg3[k][:, s, :, :].rearrange("p a r -> p (a r)"), identity16[:, :],
                                   start=True, stop=True)
                mm.then_inc(hgT_done[k], 1)

            def base(wait, k, off):
                wait(xT_ready[k], off)
                for s in range(S):
                    for c in range(ND):
                        mm = pe.matmul(acc[:, s, :], XT[k][:, c, s * P:(s + 1) * P], W_FFN[:, c, 0:D],
                                       start=s % 2 == 0 and c == 0, stop=False, skip_group_check=True)
                mm.then_inc(base_done[k], 1)

            def up(wait, k, off):
                wait(hgT_kept[k], off)
                for s in range(S):
                    mm = pe.matmul(acc[:, s, :], hgT[:, s * P:(s + 1) * P], W_UP[:, :],
                                   start=False, stop=True, skip_group_check=True)
                mm.then_inc(ffn_done[k], 1)

            def o_transposes(wait, r):
                h, part = divmod(r, 2)
                if part == 0:
                    wait(pv_dve[h], PROJ_OUT)
                    wait(pv_pool[h], PROJ_OUT)
                for q in range(2):
                    for i in range(S):
                        c = 2 * part + q
                        mm = pe.transpose(tp[:, q, i * P:(i + 1) * P], O[h][:, i, c * P:(c + 1) * P],
                                          identity[:, :])
                mm.then_inc(oT_done[r], 1)

            def out_project(wait, s):
                if s == 0:
                    for r in range(4):
                        wait(oT_kept[r], PROJ_OUT)
                n = 0
                for c in range(NF):
                    for o, w in ((OT_HI, W_OUT_HI), (OT_HI, W_OUT_LO), (OT_LO, W_OUT_HI)):
                        mm = pe.matmul(acc[:, s, :], o[:, c, s * P:(s + 1) * P], w[:, c, :],
                                       start=n == 0, stop=n == 3 * NF - 1)
                        n += 1
                if s == S - 1:
                    mm.then_inc(out_done, 1)

            def value_of_key_0(wait):
                wait(xlT_ready, TAIL)
                for c in range(ND):
                    mm = pe.matmul(acc[:, 0, :], XLT[:, c, 0, :], W_VO[:, c, :], start=c == 0,
                                   stop=c == ND - 1)
                mm.then_inc(vo_done, 1)

            def slot(t, at, par, n):
                wait, wait_ends = waiter(pe, t, at)
                head, tail, mix, proj, last = stages(t)
                if mix:
                    if t == 0:
                        pe.wait_ge(weights_ready, 4)
                    qkv_group(wait, par, 0)
                    qkv_group(wait, par, 1)
                    qkv_group(wait, par, 2)
                    qkv_group(wait, par, 3)
                if last:
                    wait(ln_rows[3], LAST)
                    wait(xlT_ready, TAIL - 1)
                    wait_ends(oT_kept[3], PROJ_OUT - 1)
                    wait_ends(hgT_kept[1], LAST - 1)
                    transposes(XN3, ln_T[3])
                    wait(ms_ready, HEAD - 1)
                    wait_ends(rest_kept[0], TAIL - 1)
                    rest(wait, 1, LAST)
                if head:
                    wait(ln_rows[0], HEAD)
                    wait(xT_ready[1], LAST)
                    wait_ends(xlT_ready, TAIL - 1)
                    wait_ends(oT_kept[3], PROJ_OUT - 1)
                    transposes(XN, ln_T[0])
                if last:
                    wait(res_ready, TAIL - 1)
                    wait_ends(x3_ready, PROJ_OUT - 1)
                    wait_ends(x1_ready, HEAD - 1)
                    base(wait, 1, LAST)
                if tail:
                    wait(ln_rows[1], TAIL)
                    wait(scanned, HEAD)
                    wait_ends(xT_ready[1], LAST)
                    wait_ends(xlT_ready, TAIL - 1)
                    transposes(XN, ln_T[1])
                if mix:
                    qkv_group(wait, par, 4)
                if tail:
                    wait(rest_kept[1], LAST)
                    wait_ends(ms_ready, HEAD - 1)
                    rest(wait, 0, TAIL)
                if mix:
                    qkv_group(wait, par, 5)
                if last:
                    wait(xT_ready[0], TAIL)
                    wait_ends(scanned, HEAD)
                    wait_ends(xT_ready[1], LAST)
                    gate_T(wait, 1, LAST)
                    up(wait, 1, LAST)
                if proj:
                    wait(hgT_kept[1], LAST)
                    wait_ends(xT_ready[0], TAIL)
                    wait_ends(scanned, HEAD)
                    o_transposes(wait, 0)
                if head:
                    wait(ffn_added[1], LAST)
                    wait_ends(res_ready, TAIL - 1)
                    wait_ends(x3_ready, PROJ_OUT - 1)
                    wait(rest_kept[0], TAIL)
                    wait_ends(rest_kept[1], LAST)
                    project(wait)
                if mix:
                    qkv_group(wait, par, 6)
                    qkv_group(wait, par, 7)
                    qkv_group(wait, par, 8)
                if proj:
                    wait(oT_kept[0], PROJ_OUT)
                    wait_ends(hgT_kept[1], LAST)
                    wait_ends(xT_ready[0], TAIL)
                    o_transposes(wait, 1)
                if tail:
                    wait(x1_ready, HEAD)
                    wait_ends(ffn_added[1], LAST)
                    wait_ends(res_ready, TAIL - 1)
                    base(wait, 0, TAIL)
                    wait(oT_kept[1], PROJ_OUT)
                    wait_ends(hgT_kept[1], LAST)
                    wait_ends(xT_ready[0], TAIL)
                    gate_T(wait, 0, TAIL)
                if mix:
                    qkv_group(wait, par, 9)
                if tail:
                    up(wait, 0, TAIL)
                if mix:
                    qkv_group(wait, par, 10)
                    qkv_group(wait, par, 11)
                if proj:
                    wait(hgT_kept[0], TAIL)
                    wait_ends(oT_kept[1], PROJ_OUT)
                    wait_ends(hgT_kept[1], LAST)
                    o_transposes(wait, 2)
                if mix:
                    qkv_group(wait, par, 12)
                    qkv_group(wait, par, 13)
                if proj:
                    wait(oT_kept[2], PROJ_OUT)
                    wait_ends(hgT_kept[0], TAIL)
                    wait_ends(hgT_kept[1], LAST)
                    o_transposes(wait, 3)
                if mix:
                    qkv_group(wait, par, 14)
                    qkv_group(wait, par, 15)
                if proj:
                    wait(ffn_added[0], TAIL)
                    wait_ends(x1_ready, HEAD)
                    wait_ends(ffn_added[1], LAST)
                    out_project(wait, 0)
                    out_project(wait, 1)
                if tail:
                    wait(ln_rows[2], TAIL)
                    wait(oT_kept[3], PROJ_OUT)
                    wait_ends(hgT_kept[0], TAIL)
                    wait_ends(hgT_kept[1], LAST)
                    transposes(XN, ln_T[2])
                if proj:
                    out_project(wait, 2)
                    out_project(wait, 3)
                if mix:
                    qkv_group(wait, par, 16)
                    qkv_group(wait, par, 17)
                if tail:
                    wait(x3_ready, PROJ_OUT)
                    wait_ends(ffn_added[0], TAIL)
                    wait_ends(x1_ready, HEAD)
                    value_of_key_0(wait)
                if mix:
                    qkv_group(wait, par, 18)
                    qkv_group(wait, par, 19)

            run_slots(pe, slot, (LAST - 1, HEAD), gains, router_weights)

        @block.scalar
        def _(act):
            def decay_exponential():
                act.wait_ge(head_loaded, 16 * N_LOADS[0])
                act.activation(decay[:, :], decay[:, :], ACT.Exp, scale=-1.0).then_inc(decay_exp, 1)

            def value_0_weights():
                act.wait_ge(temp_clamped, 1)
                act.activation(TEMP[:, :], TEMP[:, :], ACT.Exp).then_inc(temp_exp, 1)
                act.wait_ge(vo_made, 1)
                act.activation(W_VO[:, :, :], tp[:, :, 0:D], ACT.Copy).then_inc(vo_kept, 1)

            def high_weights():
                act.wait_ge(w_staged, 48)
                for c in range(3):
                    act.activation(W_HI[:, :, c * F:(c + 1) * F], stage_qkv[c], ACT.Copy, scale=W_SCALE
                                   ).then_inc(w_high, 1)
                act.wait_ge(out_loaded, 16 * N_LOADS[1])
                act.activation(W_OUT_HI[:, 0:6, :], stage_out[0], ACT.Copy, scale=W_SCALE)
                act.activation(W_OUT_HI[:, 6:NF, :], stage_out[1], ACT.Copy, scale=W_SCALE
                               ).then_inc(w_high, 1)

            def rows(wait, src, dst, k, off):
                wait(ln_scale[k], off)
                for s in range(S):
                    a = act.activation(dst[:, s, :], src[:, s, :], ACT.Identity, scale=RS[k][:, s:s + 1],
                                       bias=NR_[k][:, s:s + 1])
                a.then_inc(ln_rows[k], 1)

            def keep_qkv(wait, g):
                h, kind, k = group(g)
                if g % (NQ // 2) == 0:
                    wait(s_ready[h], MIX - 1)
                if kind == "v" and k == 0:
                    wait(pv_dve[h], MIX - 1)
                    wait(pv_pool[h], MIX - 1)
                wait(qkv_done[g], MIX)
                dst = {"q": Q, "k": K, "v": V}[kind][h][:, k, :]
                act.activation(dst, qkv_ps[g % 3][:, :], ACT.Copy,
                               scale=(O_SCALE if kind == "v" else 1.0) / W_SCALE
                               ).then_inc(qkv_kept[g], 1)

            def squares(wait):
                wait(scanned, HEAD)
                for c in range(ND):
                    a = act.activation(YSQ[:, c, :], Y[:, c, :, :].rearrange("p s t -> p (s t)"),
                                       ACT.Square, scale=c_gain[:, c:c + 1])
                a.then_inc(squared, 1)

            def keep_T(wait, k, off):
                wait(ln_T[1 if k == 0 else 3], off)
                if k == 0:
                    wait(ffn_done[0], off - 1)
                for c in range(ND):
                    a = act.activation(XT[k][:, c, :], tp[:, c, :], ACT.Copy)
                a.then_inc(xT_ready[k], 1)

            def norms(wait, k, off):
                wait(rest_kept[k], off)
                wait(n2_ready[k], off - 1)
                for s in range(S):
                    a = act.activation(junk[k][:, s, :], G[k]["rest"][:, s, 0:PROJ], ACT.Square,
                                       accum_out=G[k]["n2"][:, s:s + 1])
                a.then_inc(n2_ready[k], 1)

            def router_exp(wait, k, off):
                wait(d_ready[k], off)
                act.activation(G[k]["e"][:, :, :], G[k]["d"][:, :, :], ACT.Exp).then_inc(e_ready[k], 1)

            def keep_gT(wait, k, off):
                wait(hgT_done[k], off)
                act.activation(hgT[:, :], tp[0:3 * UP, 0, :], ACT.Copy).then_inc(hgT_kept[k], 1)

            def high_oT(wait, r):
                wait(oT_done[r], PROJ_OUT)
                if r == 0:
                    wait(out_done, PROJ_OUT - 1)
                for q in range(2):
                    a = act.activation(OT_HI[:, 2 * r + q, :], tp[:, q, :], ACT.Copy)
                a.then_inc(oT_high[r], 1)

            def softmax_exp(wait, h, off):
                wait(s_ready[h], off)
                act.activation(SE[h][:, :, :, :], SD[h][:, :, :, :], ACT.Exp, scale=SM_SCALE
                               ).then_inc(exp_ready[h], 1)

            def attn_b_rows(wait, xa):
                wait(ln_scale[2], TAIL)
                for s in range(S):
                    a = act.activation(XN[:, s, :], xa[:, s, :], ACT.Identity,
                                       scale=R12[:, s:s + 1], bias=NR12[:, s:s + 1])
                a.then_inc(ln_rows[2], 1)

            def residual(wait, xa, r):
                wait(ln_scale[2], TAIL)
                wait(x3_ready, PROJ_OUT)
                for s in range(S):
                    a = act.activation(r[:, s, :], xa[:, s, :], ACT.Identity,
                                       scale=R1P[:, s:s + 1], bias=NR_[2][:, s:s + 1])
                a.then_inc(res_scaled, 1)

            def keep_xlT(wait):
                wait(ln_T[2], TAIL)
                for c in range(ND):
                    a = act.activation(XLT[:, c, :, :].rearrange("p s t -> p (s t)"), tp[:, c, :],
                                       ACT.Identity, scale=LNWB[:, 0, c:c + 1],
                                       bias=LNWB[:, 1, c:c + 1])
                a.then_inc(xlT_ready, 1)

            def high_x(wait, xh):
                wait(xlT_ready, TAIL)
                act.activation(xh[:, :, :, :], XLT[:, :, :, :], ACT.Copy).then_inc(xh_ready, 1)

            def high_d(wait, dh):
                wait(xd_ready, TAIL)
                act.activation(dh[:, :, :, :], XD[:, :, :, :], ACT.Copy).then_inc(dh_ready, 1)

            def slot(t, at, par, n):
                wait, wait_ends = waiter(act, t, at)
                head, tail, mix, proj, last = stages(t)
                if mix:
                    keep_qkv(wait, 0)
                    keep_qkv(wait, 1)
                if last:
                    rows(wait, X3, XN3, 3, LAST)
                    keep_T(wait, 1, LAST)
                if head:
                    wait(ln_T[2], TAIL - 1)
                    wait_ends(projected, HEAD - 1)
                    rows(wait, X[par], XN, 0, HEAD)
                if mix:
                    keep_qkv(wait, 2)
                if last:
                    norms(wait, 1, LAST)
                if tail:
                    wait(ln_T[0], HEAD)
                    wait_ends(ln_T[2], TAIL - 1)
                    rows(wait, X[1 - par], XN, 1, TAIL)
                if last:
                    router_exp(wait, 1, LAST)
                if mix:
                    keep_qkv(wait, 3)
                if tail:
                    keep_T(wait, 0, TAIL)
                if head:
                    wait(ln_T[1], TAIL)
                    wait_ends(ln_T[0], HEAD)
                    squares(wait)
                if proj:
                    softmax_exp(wait, 1, PROJ_OUT)
                if tail:
                    norms(wait, 0, TAIL)
                if last:
                    wait(ffn_done[0], TAIL - 1)
                    keep_gT(wait, 1, LAST)
                if mix:
                    keep_qkv(wait, 4)
                if proj:
                    high_oT(wait, 0)
                if mix:
                    keep_qkv(wait, 5)
                if tail:
                    router_exp(wait, 0, TAIL)
                if mix:
                    keep_qkv(wait, 6)
                    keep_qkv(wait, 7)
                    keep_qkv(wait, 8)
                if proj:
                    high_oT(wait, 1)
                if tail:
                    wait(ffn_done[1], LAST)
                    keep_gT(wait, 0, TAIL)
                    if t == FIRST_SLOT + 1:
                        high_weights()
                if mix:
                    keep_qkv(wait, 9)
                    keep_qkv(wait, 10)
                if proj:
                    high_oT(wait, 2)
                if mix:
                    keep_qkv(wait, 11)
                    keep_qkv(wait, 12)
                    keep_qkv(wait, 13)
                if proj:
                    high_oT(wait, 3)
                if mix:
                    softmax_exp(wait, 0, MIX)
                if tail:
                    wait(projected, HEAD)
                    wait_ends(ln_T[1], TAIL)
                    attn_b_rows(wait, X[1 - par])
                if mix:
                    keep_qkv(wait, 14)
                    keep_qkv(wait, 15)
                if tail:
                    keep_xlT(wait)
                    residual(wait, X[1 - par], R[1 - par])
                    high_d(wait, DHI[1 - par])
                if mix:
                    keep_qkv(wait, 16)
                    keep_qkv(wait, 17)
                if tail:
                    high_x(wait, XH[1 - par])
                if mix:
                    keep_qkv(wait, 18)
                    keep_qkv(wait, 19)

            run_slots(act, slot, (LAST - 1, HEAD), decay_exponential, value_0_weights)

        @block.gpsimd
        def _(pool):
            steps = [0]

            def link(ins):
                steps[0] += 1
                ins.then_inc(pool_step, 1)
                pool.wait_ge(pool_step, steps[0])

            def restart():
                pool.sem_clear(pool_step)
                steps[0] = 0

            def settle():
                pool.wait_ge(halves_set, 1)

            pool.memset(m_one[:, :], -1.0)
            for k in range(2):
                pool.memset(G[k]["cu"][:, :, 0:1], 1.0)
                pool.memset(hg3[k][:, :, :, :], 0.0)
            pool.memset(m_half[:, :], -0.5).then_inc(halves_set, 1)

            def sim_scales():
                settle()
                pool.wait_ge(sim_norm2, 1)
                pool.tensor_tensor(SIMI[:, :], SIM2[:, :], m_half[0:PROJ, :], ALU.pow).then_inc(sim_scale, 1)

            def row_scale(wait, k, off):
                settle()
                wait(ln_var[k], off)
                link(pool.tensor_tensor(RS[k][:, :], VE[k][:, :], m_half[:, :], ALU.pow))
                pool.tensor_tensor(NR_[k][:, :], NM[k][:, :], RS[k][:, :], ALU.mult
                                   ).then_inc(ln_scale[k], 1)

            def router_logits(wait, k, off):
                g = G[k]
                settle()
                wait(n2_ready[k], off)
                link(pool.tensor_scalar(g["nc"][:, :], g["n2"][:, :], 1e-24, None, ALU.max))
                link(pool.tensor_tensor(g["ni"][:, :], g["nc"][:, :], m_half[:, :], ALU.pow))
                pool.tensor_tensor(g["lg"][:, :, :], g["rest"][:, :, PROJ + NR:REST],
                                   g["ni"][:, :, None].broadcast_to([P, S, NE]), ALU.mult
                                   ).then_inc(lg_ready[k], 1)

            def router_choice(wait, k, off):
                g = G[k]
                settle()
                wait(d_ready[k], off)
                d, cu, ne = g["d"], g["cu"], g["ne"]
                pool.tensor_scalar(g["eq"][:, :, :], d[:, :, :], 0.0, None, ALU.is_ge)
                pool.tensor_scalar(ne[:, :, :], d[:, :, 1:3], 0.0, None, ALU.is_lt)
                link(pool.tensor_scalar(cu[:, :, 1:2], d[:, :, 0:1], 0.0, None, ALU.is_lt))
                link(pool.tensor_tensor(cu[:, :, 2:3], cu[:, :, 1:2], ne[:, :, 0:1], ALU.mult))
                link(pool.tensor_tensor(cu[:, :, 3:4], cu[:, :, 2:3], ne[:, :, 1:2], ALU.mult))
                link(pool.tensor_tensor(g["sel"][:, :, :], g["eq"][:, :, :], cu[:, :, :], ALU.mult))

            def router_gate(wait, k, off):
                g = G[k]
                settle()
                wait(e_ready[k], off)
                link(pool.tensor_tensor(g["s2"][:, :, :], g["e"][:, :, 0:2], g["e"][:, :, 2:4], ALU.add))
                link(pool.tensor_tensor(g["s1"][:, :, :], g["s2"][:, :, 0:1], g["s2"][:, :, 1:2], ALU.add))
                link(pool.tensor_tensor(g["si"][:, :, 0], g["s1"][:, :, 0], m_one[:, :], ALU.pow))
                link(pool.tensor_tensor(g["ge"][:, :, :], g["e"][:, :, :], g["sel"][:, :, :], ALU.mult))
                link(pool.tensor_tensor(g["g"][:, :, :], g["ge"][:, :, :],
                                        g["si"][:, :, :].broadcast_to([P, S, NE]), ALU.mult))
                settle()
                wait(hgT_done[k], off - 1)
                lo = 0
                for e, r in enumerate(RANKS):
                    last = pool.tensor_tensor(g["hg"][:, :, lo:lo + r],
                                              g["rest"][:, :, PROJ + lo:PROJ + lo + r],
                                              g["g"][:, :, e:e + 1].broadcast_to([P, S, r]), ALU.mult)
                    lo += r
                link(last)
                link(pool.tensor_scalar(hg3[k][:, :, 0:2, 0:NR],
                                        g["hg"][:, :, None, :].broadcast_to([P, S, 2, NR]), 1.0, None,
                                        ALU.mult))
                pool.tensor_tensor(hg3[k][:, :, 2, 0:NR], g["hg"][:, :, :], hg3[k][:, :, 0, 0:NR],
                                   ALU.subtract).then_inc(hg_ready[k], 1)

            def qk(wait, h, off):
                settle()
                wait(qkv_kept[gk(h)], off)
                wait(qkv_kept[gq(h, 3)], off)
                pool.tensor_tensor(PS[:, :, :], K[h][:, :, :],
                                   Q[h][:, 3:4, :].broadcast_to([P, NKEY, FH]), ALU.mult
                                   ).then_inc(qk_pool[h], 1)

            def pv(wait, h, off, i):
                settle()
                if i == 2:
                    wait(p_ready[h], off)
                    wait(qkv_kept[gv(h)], off)
                    wait(oT_done[2 * h + 1], off - 1)
                    if h == 1:
                        wait(ffn_done[1], off - 1)
                link(pool.tensor_tensor(
                    PV[:, :, :].rearrange("p j (g d) -> p j g d", g=HH),
                    V[h][:, :, :].rearrange("p j (g d) -> p j g d", g=HH),
                    PR[h][:, i, :, :, None].broadcast_to([P, NKEY, HH, DH]), ALU.mult))
                link(pool.tensor_tensor(O[h][:, i, :], PV[:, 0, :], PV[:, 1, :], ALU.add))
                add = pool.tensor_tensor(O[h][:, i, :], O[h][:, i, :], PV[:, 2, :], ALU.add)
                if i == 2:
                    link(add)
                else:
                    add.then_inc(pv_pool[h], 1)
                    settle()
                    wait(pv_pool[h], off)

            def sum_of_squares(wait):
                settle()
                wait(squared, HEAD)
                pool.tensor_tensor(YSQ[:, 0, :], YSQ[:, 0, :], YSQ[:, 1, :], ALU.add
                                   ).then_inc(squares_summed, 1)

            def rms_scale(wait):
                settle()
                wait(ms_ready, HEAD)
                pool.tensor_tensor(RMS[:, :], MS[:, :], m_half[:, :], ALU.pow).then_inc(rms_ready, 1)

            def attn_b_scales(wait):
                settle()
                wait(ln_var[2], TAIL)
                link(pool.tensor_tensor(RS[2][:, :], VE[2][:, :], m_half[:, :], ALU.pow))
                link(pool.tensor_tensor(NR_[2][:, :], NM[2][:, :], RS[2][:, :], ALU.mult))
                link(pool.tensor_scalar(R1P[:, :], RS[2][:, :], 1.0, None, ALU.add))
                link(pool.tensor_tensor(B1[:, :], MV[2][:, :, 1], RS[2][:, :], ALU.mult))
                link(pool.tensor_tensor(B2[:, :], B1[:, :], RS[2][:, :], ALU.mult))
                link(pool.tensor_scalar(B3[:, :], B2[:, :], LN_EPS, None, ALU.add))
                link(pool.tensor_tensor(B1[:, :], B3[:, :], m_half[:, :], ALU.pow))
                link(pool.tensor_tensor(R12[:, :], RS[2][:, :], B1[:, :], ALU.mult))
                pool.tensor_tensor(NR12[:, :], NM[2][:, :], R12[:, :], ALU.mult).then_inc(ln_scale[2], 1)

            def differences(wait):
                settle()
                wait(xlT_ready, TAIL)
                wait(dl_ready, TAIL - 1)
                pool.tensor_tensor(XD[:, :, :, :], XLT[:, :, 1:S, :],
                                   XLT[:, :, 0:1, :].broadcast_to([P, ND, NKEY, P]), ALU.subtract
                                   ).then_inc(xd_ready, 1)

            def low_x(wait, xl, xh):
                settle()
                wait(xh_ready, TAIL)
                pool.tensor_tensor(xl[:, :, :, :], XLT[:, :, :, :], xh[:, :, :, :], ALU.subtract
                                   ).then_inc(xl_ready, 1)

            def low_d(wait, dl, dh):
                settle()
                wait(dh_ready, TAIL)
                pool.tensor_tensor(dl[:, :, :, :], XD[:, :, :, :], dh[:, :, :, :], ALU.subtract
                                   ).then_inc(dl_ready, 1)

            def slot(t, at, par, n):
                wait, wait_ends = waiter(pool, t, at)
                head, tail, mix, proj, last = stages(t)
                if last:
                    row_scale(wait, 3, LAST)
                if head:
                    row_scale(wait, 0, HEAD)
                if tail:
                    row_scale(wait, 1, TAIL)
                if proj:
                    wait(s_ready[0], MIX - 1)
                    qk(wait, 1, PROJ_OUT)
                if last:
                    router_logits(wait, 1, LAST)
                    router_choice(wait, 1, LAST)
                    router_gate(wait, 1, LAST)
                if head:
                    sum_of_squares(wait)
                if tail:
                    router_logits(wait, 0, TAIL)
                if proj:
                    pv(wait, 1, PROJ_OUT, 2)
                if head:
                    rms_scale(wait)
                if tail:
                    router_choice(wait, 0, TAIL)
                    router_gate(wait, 0, TAIL)
                if proj:
                    pv(wait, 1, PROJ_OUT, 3)
                if mix:
                    wait(s_ready[1], PROJ_OUT)
                    qk(wait, 0, MIX)
                if tail:
                    attn_b_scales(wait)
                if mix:
                    pv(wait, 0, MIX, 2)
                if tail:
                    differences(wait)
                if mix:
                    pv(wait, 0, MIX, 3)
                if tail:
                    low_d(wait, DLO[1 - par], DHI[1 - par])
                    low_x(wait, XL[1 - par], XH[1 - par])
                restart()

            run_slots(pool, slot, (LAST - 1, HEAD), None, sim_scales)

        @block.vector
        def _(dve):
            steps = [0]

            def mark(ins):
                steps[0] += 1
                ins.then_inc(dve_step, 1)
                return steps[0]

            def link(ins):
                dve.wait_ge(dve_step, mark(ins))

            def restart():
                dve.wait_ge(dve_step, steps[0])
                dve.sem_clear(dve_step)
                steps[0] = 0

            def head_weights():
                mark(dve.memset(ones[:, :], 1.0))
                mark(dve.memset(carry[:, :, :], 0.0))
                dve.wait_ge(head_loaded, 16 * N_LOADS[0])
                dve.tensor_tensor(qk_prod[:, :], qk_in[:, 0, :], qk_in[:, 1, :], ALU.mult
                                  ).then_inc(qk_multiplied, 1)
                dve.wait_ge(decay_exp, 1)
                link(dve.tensor_scalar(decay[:, :], decay[:, :], 1.0, None, ALU.add))
                link(dve.reciprocal(decay[:, :], decay[:, :]))
                dve.wait_ge(gain_summed, 1)
                link(dve.tensor_copy(c_gain[:, :], small[:, 0:ND]))
                link(dve.tensor_tensor(cnw[:, :], c_gain[:, :], nw[:, :], ALU.mult))
                for c in range(ND):
                    a = dve.tensor_scalar(WO_A[:, c, :], WO_A[:, c, :], cnw[:, c:c + 1], None, ALU.mult)
                a.then_inc(head_ready, 1)
                for h in range(2):
                    mark(dve.memset(SC[h][:, :, :, :], 0.0))
                mark(dve.memset(BROW[:, PROJ:REST], 0.0))
                mark(dve.memset(W_UP[:, :], 0.0))
                mark(dve.tensor_copy(identity16[:, :], identity[:, :]))
                restart()

            def ffn_weights():
                dve.wait_ge(ffn_loaded, 16 * N_LOADS[2])
                dve.tensor_scalar(TEMP[:, :], TEMP[:, :], CLAMP_MAX, None, ALU.min).then_inc(temp_clamped, 1)
                dve.tensor_tensor(SIM2[:, :], SIM[:, :], SIM[:, :], ALU.mult).then_inc(sim_squared, 1)
                mark(dve.tensor_scalar(BPB, ones[0:PROJ, :], BP[:, 0:1], None, ALU.mult))
                for i in range(3):
                    last = mark(dve.tensor_scalar(W_UP[UP * i:UP * i + NR, :],
                                                  up_stage[UP * i:UP * i + NR, :], W_SCALE, None, ALU.mult))
                dve.wait_ge(dve_step, last)
                mark(dve.scalar_tensor_tensor(W_UP[UP:UP + NR, :], up_stage[UP:UP + NR, :], W_SCALE,
                                              W_UP[UP:UP + NR, :], ALU.mult, ALU.subtract))
                mark(dve.tensor_scalar(W_FFN[:, :, 0:D], W_FFN[:, :, 0:D], W_SCALE, None, ALU.mult))
                dve.wait_ge(sim_summed, 1)
                dve.tensor_scalar(SIM2[:, :], small[0:PROJ, 8:8 + NE], 1e-24, None, ALU.max
                                  ).then_inc(sim_norm2, 1)
                dve.wait_ge(sim_scale, 1)
                link(dve.tensor_tensor(SIMI[:, :], SIM[:, :], SIMI[:, :], ALU.mult))
                dve.wait_ge(temp_exp, 1)
                dve.tensor_scalar(SIMI[:, :], SIMI[:, :], TEMP[:, 0:1], None, ALU.mult).then_inc(sim_ready, 1)
                dve.wait_ge(router_made, 1)
                for c in range(ND):
                    mark(dve.tensor_copy(W_FFN[:, c, D + PROJ + NR:D + REST],
                                         small[:, 16 + NE * c:16 + NE * (c + 1)]))
                dve.tensor_copy(BROW[:, PROJ + NR:REST], small[:, 32:32 + NE]).then_inc(ffn_ready, 1)
                dve.wait_ge(ffn_ready, 1)
                restart()

            def low_weights():
                for c in range(3):
                    dve.wait_ge(w_high, c + 1)
                    dve.scalar_tensor_tensor(W_LO[:, :, c * F:(c + 1) * F], stage_qkv[c], W_SCALE,
                                             W_HI[:, :, c * F:(c + 1) * F], ALU.mult, ALU.subtract
                                             ).then_inc(weights_ready, 1)
                dve.wait_ge(w_high, 4)
                mark(dve.scalar_tensor_tensor(W_OUT_LO[:, 0:6, :], stage_out[0], W_SCALE,
                                              W_OUT_HI[:, 0:6, :], ALU.mult, ALU.subtract))
                dve.scalar_tensor_tensor(W_OUT_LO[:, 6:NF, :], stage_out[1], W_SCALE,
                                         W_OUT_HI[:, 6:NF, :], ALU.mult, ALU.subtract
                                         ).then_inc(weights_ready, 1)

            def statistics(src, k):
                for s in range(S):
                    last = mark(dve.bn_stats(BS[k][:, s, :], src[:, s, :]))
                dve.wait_ge(dve_step, last)
                for s in range(S):
                    last = mark(dve.bn_aggr(MV[k][:, s, :], BS[k][:, s, :]))
                dve.wait_ge(dve_step, last)
                mark(dve.tensor_scalar(NM[k][:, :], MV[k][:, :, 0], -1.0, None, ALU.mult))
                dve.tensor_scalar(VE[k][:, :], MV[k][:, :, 1], LN_EPS, None, ALU.add
                                  ).then_inc(ln_var[k], 1)

            def head_statistics(xa, par, n):
                dve.wait_ge(x_loaded[par], n * 8 + 8 * (4 - par))
                statistics(xa, 0)

            def ffn1_statistics(wait, xa):
                wait(x1_ready, HEAD)
                wait(ln_scale[1], HEAD - 1)
                statistics(xa, 1)

            def attn_b_statistics(wait, xa):
                wait(ffn_added[0], TAIL)
                statistics(xa, 2)

            def ffn2_statistics(wait):
                wait(x3_ready, LAST)
                statistics(X3, 3)

            def scan(wait):
                wait(ln_T[0], HEAD)
                wait(projected, HEAD - 1)
                wait(scanned, HEAD - 1)
                for s in range(S):
                    for c in range(ND):
                        a = mark(dve.tensor_tensor_scan(
                            Y[:, c, s, :], decay[:, c:c + 1].broadcast_to([P, P]),
                            tp[:, c, s * P:(s + 1) * P], carry[:, c, s:s + 1], ALU.mult, ALU.add))
                dve.wait_ge(dve_step, a)
                dve.tensor_copy(carry[:, :, :], Y[:, :, :, P - 1]).then_inc(scanned, 1)

            def mean_square(wait):
                wait(projected, HEAD)
                dve.tensor_scalar(MS[:, :], ssq_ps, 1.0 / D, RMS_EPS, ALU.mult, ALU.add
                                  ).then_inc(ms_ready, 1)

            def add_attn_a(wait, xa):
                wait(rms_ready, HEAD)
                wait(projected, HEAD)
                for s in range(S):
                    a = dve.scalar_tensor_tensor(xa[:, s, :], acc[:, s, :], RMS[:, s:s + 1],
                                                 xa[:, s, :], ALU.mult, ALU.add)
                a.then_inc(x1_ready, 1)

            def keep_rest(wait, k, off):
                wait(rest_done[k], off)
                dve.tensor_tensor(G[k]["rest"][:, :, :], rest_ps[:, :, :],
                                  BROW[:, None, :].broadcast_to([P, S, REST]), ALU.add
                                  ).then_inc(rest_kept[k], 1)

            def maximum(wait, k, off):
                wait(lg_ready[k], off)
                link(dve.tensor_reduce(G[k]["m"][:, :], G[k]["lg"][:, :, :], AX.X, ALU.max))
                dve.tensor_tensor(G[k]["d"][:, :, :], G[k]["lg"][:, :, :],
                                  G[k]["m"][:, :, None].broadcast_to([P, S, NE]), ALU.subtract
                                  ).then_inc(d_ready[k], 1)

            def add_ffn(wait, x, k, off):
                wait(ffn_done[k], off)
                dve.scalar_tensor_tensor(x[:, :, :], acc[:, :, :], 1.0 / W_SCALE, x[:, :, :],
                                         ALU.mult, ALU.add).then_inc(ffn_added[k], 1)

            def add_attn_b(wait, r, n, t):
                wait(out_done, PROJ_OUT)
                wait(res_ready, PROJ_OUT)
                if t is None or t >= 2:
                    dve.wait_ge(stored, (n - 1) * 16)
                dve.scalar_tensor_tensor(X3[:, :, :], acc[:, :, :], 1.0 / (W_SCALE * O_SCALE), r[:, :, :],
                                         ALU.mult, ALU.add).then_inc(x3_ready, 1)

            def low_oT(wait, r):
                wait(oT_high[r], PROJ_OUT)
                if r == 0:
                    wait(out_done, PROJ_OUT - 1)
                dve.tensor_tensor(OT_LO[:, 2 * r:2 * r + 2, :], tp[:, :, :], OT_HI[:, 2 * r:2 * r + 2, :],
                                  ALU.subtract).then_inc(oT_kept[r], 1)

            def add_value_0(wait, r):
                wait(vo_done, TAIL)
                wait(res_scaled, TAIL)
                dve.tensor_tensor(r[:, :, :], r[:, :, :], acc[:, 0:1, :].broadcast_to([P, S, D]), ALU.add
                                  ).then_inc(res_ready, 1)

            made = {}
            used = [0, 0, 0]

            def product(wait, h, off, i):
                if i == 0:
                    wait(qkv_kept[gk(h)], off)
                wait(qkv_kept[gq(h, i)], off)
                if used[i]:
                    dve.wait_ge(dve_step, used[i])
                made[h, i] = mark(dve.tensor_tensor(
                    PD[i][:, :, :], K[h][:, :, :], Q[h][:, i:i + 1, :].broadcast_to([P, NKEY, FH]),
                    ALU.mult))

            def total(wait, h, off, i):
                if i == 3:
                    wait(qk_pool[h], off)
                else:
                    dve.wait_ge(dve_step, made[h, i])
                src = PS if i == 3 else PD[i]
                step = mark(dve.tensor_reduce(SC[h][:, i, 1:4, :], src[:, :, :].rearrange(
                    "p j (g d) -> p j g d", g=HH), AX.X, ALU.add))
                made[h, "total"] = step
                if i < 3:
                    used[i] = step

            def below_maximum(wait, h, off):
                dve.wait_ge(dve_step, made[h, "total"])
                link(dve.tensor_reduce(SM[h][:, :, :], SC[h][:, :, :, :].rearrange("p i j g -> p i g j"),
                                       AX.X, ALU.max))
                dve.tensor_tensor(SD[h][:, :, :, :], SC[h][:, :, :, :],
                                  SM[h][:, :, None, :].broadcast_to([P, S, 4, HH]), ALU.subtract
                                  ).then_inc(s_ready[h], 1)

            def probabilities(wait, h, off):
                wait(exp_ready[h], off)
                link(dve.tensor_reduce(SS[h][:, :, :], SE[h][:, :, :, :].rearrange("p i j g -> p i g j"),
                                       AX.X, ALU.add))
                link(dve.reciprocal(SI[h][:, :, :], SS[h][:, :, :]))
                dve.tensor_tensor(PR[h][:, :, :, :], SE[h][:, :, 1:4, :],
                                  SI[h][:, :, None, :].broadcast_to([P, S, NKEY, HH]), ALU.mult
                                  ).then_inc(p_ready[h], 1)

            def pv(wait, h, off, i):
                if i == 0:
                    wait(p_ready[h], off)
                    wait(qkv_kept[gv(h)], off)
                    wait(oT_done[2 * h + 1], off - 1)
                    if h == 1:
                        wait(ffn_done[1], off - 1)
                if used[i]:
                    dve.wait_ge(dve_step, used[i])
                link(dve.tensor_tensor(
                    PD[i][:, :, :].rearrange("p j (g d) -> p j g d", g=HH),
                    V[h][:, :, :].rearrange("p j (g d) -> p j g d", g=HH),
                    PR[h][:, i, :, :, None].broadcast_to([P, NKEY, HH, DH]), ALU.mult))
                link(dve.tensor_tensor(PD[i][:, 0, :], PD[i][:, 0, :], PD[i][:, 1, :], ALU.add))
                a = dve.tensor_tensor(O[h][:, i, :], PD[i][:, 0, :], PD[i][:, 2, :], ALU.add)
                if i == 0:
                    used[i] = mark(a)
                else:
                    a.then_inc(pv_dve[h], 1)
                    wait(pv_dve[h], off)

            def slot(t, at, par, n):
                wait, wait_ends = waiter(dve, t, at)
                head, tail, mix, proj, last = stages(t)
                used[:] = [0, 0, 0]
                if last:
                    ffn2_statistics(wait)
                if proj:
                    product(wait, 1, PROJ_OUT, 0)
                    product(wait, 1, PROJ_OUT, 1)
                if head:
                    head_statistics(X[par], par, n)
                if proj:
                    product(wait, 1, PROJ_OUT, 2)
                    total(wait, 1, PROJ_OUT, 0)
                if last:
                    keep_rest(wait, 1, LAST)
                if proj:
                    total(wait, 1, PROJ_OUT, 1)
                if head:
                    scan(wait)
                if last:
                    maximum(wait, 1, LAST)
                if proj:
                    total(wait, 1, PROJ_OUT, 2)
                    total(wait, 1, PROJ_OUT, 3)
                    below_maximum(wait, 1, PROJ_OUT)
                if tail:
                    keep_rest(wait, 0, TAIL)
                if proj:
                    probabilities(wait, 1, PROJ_OUT)
                if mix:
                    product(wait, 0, MIX, 0)
                if last:
                    add_ffn(wait, X3, 1, LAST)
                if mix:
                    total(wait, 0, MIX, 0)
                    product(wait, 0, MIX, 1)
                if tail:
                    maximum(wait, 0, TAIL)
                if proj:
                    low_oT(wait, 0)
                if head:
                    mean_square(wait)
                if mix:
                    total(wait, 0, MIX, 1)
                if head:
                    add_attn_a(wait, X[par])
                if proj:
                    pv(wait, 1, PROJ_OUT, 0)
                    low_oT(wait, 1)
                if mix:
                    product(wait, 0, MIX, 2)
                if proj:
                    pv(wait, 1, PROJ_OUT, 1)
                if mix:
                    total(wait, 0, MIX, 2)
                if tail:
                    add_ffn(wait, X[1 - par], 0, TAIL)
                if proj:
                    low_oT(wait, 2)
                if tail:
                    attn_b_statistics(wait, X[1 - par])
                    if t == FIRST_SLOT + 1:
                        low_weights()
                if proj:
                    low_oT(wait, 3)
                if mix:
                    total(wait, 0, MIX, 3)
                    below_maximum(wait, 0, MIX)
                    probabilities(wait, 0, MIX)
                    pv(wait, 0, MIX, 0)
                    pv(wait, 0, MIX, 1)
                if proj:
                    add_attn_b(wait, R[1 - par], n, t)
                if head:
                    ffn1_statistics(wait, X[par])
                if tail:
                    add_value_0(wait, R[1 - par])
                restart()

            run_slots(dve, slot, (LAST - 1, HEAD), head_weights, ffn_weights)


_IN = ["x", "ident", "same_head", "log_decay", "qk", "norm_w", "o_wT", "w_qkvT", "w_v", "w_outT", "ln_wb",
       "w_ffnT", "w_p", "b_p", "b_row", "sim", "temp", "w_up"]


def kernel(**inputs):
    import numpy as np
    import concourse.bacc as bacc
    from concourse.bass_utils import run_bass_kernel_spmd

    a = {k.replace("L0_", ""): np.asarray(v) for k, v in inputs.items()}

    def columns(m):
        return m.reshape(-1, P, m.shape[-1]).transpose(1, 0, 2)

    def features(v):
        return v.reshape(-1, P).T

    w = a["attn_b_w_qkv"].reshape(NHEAD, 3, DH, D)
    parts = [w[:, k].reshape(F, D) for k in range(3)]
    dh = D // NHEAD
    arrays = {
        "x": a["attn_a_x"],
        "ident": np.eye(P, dtype=np.float32),
        "same_head": np.kron(np.eye(P // dh, dtype=np.float32), np.ones((dh, dh), np.float32)),
        "log_decay": features(np.repeat(a["attn_a_log_decay"], dh)),
        "qk": np.stack([features(a["attn_a_q"]), features(a["attn_a_k"])], 1),
        "norm_w": features(a["attn_a_norm_weight"]),
        "o_wT": columns(a["attn_a_o_w"].T),
        "w_qkvT": columns(np.concatenate(parts, 0).T),
        "w_v": columns(parts[2]),
        "w_outT": columns(a["attn_b_w_out"].T),
        "ln_wb": np.stack([features(a["attn_b_ln_w"]), features(a["attn_b_ln_b"])], 1),
        "w_ffnT": columns(np.concatenate([a["ffn_W"], a["ffn_Wp"]] + [a[f"ffn_Wd{e}"] for e in range(NE)]).T),
        "w_p": a["ffn_Wp"],
        "b_p": a["ffn_bp"][:, None],
        "b_row": a["ffn_bp"][None, :],
        "sim": a["ffn_sim"],
        "temp": a["ffn_temp"][None, :],
        "w_up": np.concatenate([a[f"ffn_Wu{e}"].T for e in range(NE)]),
    }
    arrays = {k: np.ascontiguousarray(v) for k, v in arrays.items()}

    nc = bacc.Bacc("TRN2", target_bir_lowering=False, num_devices=1)
    args = [nc.dram_tensor(f"in_{k}", arrays[k].shape, mybir.dt.from_np(arrays[k].dtype),
                           kind="ExternalInput").ap() for k in _IN]
    out = nc.dram_tensor("out_x", arrays["x"].shape, F32, kind="ExternalOutput").ap()
    token_mixer_stack(nc, args[0], out, *args[1:])
    r = run_bass_kernel_spmd(nc, [{f"in_{k}": arrays[k] for k in _IN}], core_ids=[0])
    return r.results[0]["out_x"]
```
